# Optimizing a Trainium2 kernel written in Bass

```python
import numpy as np
import jax
import jax.numpy as jnp

def _softmax(x, axis=-1):
    return jax.nn.softmax(x, axis=axis)

def _gelu(x):
    return jax.nn.gelu(x, approximate=True)

def _silu(x):
    return jax.nn.silu(x)

def _sigmoid(x):
    return jax.nn.sigmoid(x)

def _layernorm(x, axis=-1, eps=1e-05):
    m = jnp.mean(x, axis=axis, keepdims=True)
    v = jnp.var(x, axis=axis, keepdims=True)
    return (x - m) / jnp.sqrt(v + eps)

def _scatter_add(tgt, idx, src, axis=0):
    return tgt.at[idx].add(src)

def _segment_sum(src, seg, n):
    return jax.ops.segment_sum(src, seg, n)
kernel_name = 'mk_macaron_d1_jaxref_r4_9fc58e'

def setup_inputs(seed: int=0):
    np.random.seed(seed)
    _w = jnp.asarray

    def _L0_attn_setup():
        import math
        import jax, jax.numpy as jnp
        import numpy as np
        N_HEAD = 16
        X_INT = -100.0
        Y_INT = 1.0
        POWER = 2
        DIVISOR = 1000.0

        def polymax(x):
            m = Y_INT / X_INT
            lin_cond = (x >= X_INT) & (x <= 0)
            x_lin = jnp.where(lin_cond, x, 0.0)
            lin = jnp.where(lin_cond, m * x_lin + Y_INT, 0.0)
            pos_cond = x > 0
            x_pos = jnp.where(pos_cond, x, 0.0)
            poly = jnp.where(pos_cond, x_pos ** POWER + Y_INT, 0.0)
            return (poly + lin) / DIVISOR
        key = jax.random.key(seed)
        k1, k2, k3 = jax.random.split(key, 3)
        B, T, C = (2, 512, 256)
        x = jax.random.normal(k1, (B, T, C), dtype=jnp.float32)
        W_attn = jax.random.normal(k2, (C, 3 * C), dtype=jnp.float32) * (1.0 / math.sqrt(C))
        W_proj = jax.random.normal(k3, (C, C), dtype=jnp.float32) * (1.0 / math.sqrt(C))
        return {'x': x, 'W_attn': W_attn, 'W_proj': W_proj}
    _L0_attn_in = _L0_attn_setup()

    def _L0_ffn_setup():
        import jax, jax.numpy as jnp
        import numpy as np
        key = jax.random.key(seed)
        k1, k2, k3, k4, k5 = jax.random.split(key, 5)
        d_in, d_out, r = (256, 256, 32)
        x = jax.random.normal(k1, (8, 2048, d_in), dtype=jnp.float32)
        W = jax.random.normal(k2, (d_out, d_in), dtype=jnp.float32) * (1.0 / np.sqrt(d_in))
        b = jax.random.normal(k3, (d_out,), dtype=jnp.float32) * 0.01
        V_r = jax.random.normal(k4, (d_in, r), dtype=jnp.float32) * (1.0 / np.sqrt(d_in))
        C = jax.random.normal(k5, (d_out, r), dtype=jnp.float32) * (1.0 / np.sqrt(r))
        return {'x': x, 'W': W, 'b': b, 'V_r': V_r, 'C': C}
    _L0_ffn_in = _L0_ffn_setup()
    _d = {'L0_attn_x': _L0_attn_in['x'], 'L0_attn_W_attn': _L0_attn_in['W_attn'], 'L0_attn_W_proj': _L0_attn_in['W_proj'], 'L0_ffn_W': _L0_ffn_in['W'], 'L0_ffn_b': _L0_ffn_in['b'], 'L0_ffn_V_r': _L0_ffn_in['V_r'], 'L0_ffn_C': _L0_ffn_in['C']}
    _x0 = _d['L0_attn_x']
    _d['L0_attn_x'] = jax.random.normal(jax.random.fold_in(jax.random.key(seed), 1), (4, 2048, 256), dtype=_x0.dtype)
    del _x0
    return _d

def reference(L0_attn_x, L0_attn_W_attn, L0_attn_W_proj, L0_ffn_W, L0_ffn_b, L0_ffn_V_r, L0_ffn_C):

    def _L0_attn_ref(x, W_attn, W_proj):
        import math
        import jax, jax.numpy as jnp
        import numpy as np
        N_HEAD = 16
        X_INT = -100.0
        Y_INT = 1.0
        POWER = 2
        DIVISOR = 1000.0

        def polymax(x):
            m = Y_INT / X_INT
            lin_cond = (x >= X_INT) & (x <= 0)
            x_lin = jnp.where(lin_cond, x, 0.0)
            lin = jnp.where(lin_cond, m * x_lin + Y_INT, 0.0)
            pos_cond = x > 0
            x_pos = jnp.where(pos_cond, x, 0.0)
            poly = jnp.where(pos_cond, x_pos ** POWER + Y_INT, 0.0)
            return (poly + lin) / DIVISOR
        B, T, C = x.shape
        H = N_HEAD
        hd = C // H
        qkv = x @ W_attn
        q, k, v = jnp.split(qkv, 3, axis=-1)
        q = q.reshape(B, T, H, hd).transpose(0, 2, 1, 3)
        k = k.reshape(B, T, H, hd).transpose(0, 2, 1, 3)
        v = v.reshape(B, T, H, hd).transpose(0, 2, 1, 3)
        att = jnp.einsum('bhid,bhjd->bhij', q, k) * (1.0 / math.sqrt(hd))
        causal = jnp.tril(jnp.ones((T, T), dtype=bool))
        att = jnp.where(causal[None, None], att, -jnp.inf)
        att = polymax(att)
        y = jnp.einsum('bhij,bhjd->bhid', att, v)
        y = y.transpose(0, 2, 1, 3).reshape(B, T, C)
        return y @ W_proj

    def _L0_ffn_ref(x, W, b, V_r, C):
        import jax, jax.numpy as jnp
        import numpy as np
        base = jnp.einsum('bsd,od->bso', x, W) + b
        correction = jnp.einsum('bsr,or->bso', jnp.einsum('bsd,dr->bsr', x, V_r), C)
        return base + correction
    x = L0_attn_x
    x = x + 0.5 * _L0_ffn_ref(_layernorm(x, axis=-1), L0_ffn_W, L0_ffn_b, L0_ffn_V_r, L0_ffn_C)
    x = x + _L0_attn_ref(_layernorm(x, axis=-1), L0_attn_W_attn, L0_attn_W_proj)
    x = x + 0.5 * _L0_ffn_ref(_layernorm(x, axis=-1), L0_ffn_W, L0_ffn_b, L0_ffn_V_r, L0_ffn_C)
    return x

_drawn_inputs = setup_inputs


def setup_inputs(seed=0):
    import zlib

    import numpy as np

    out = dict(_drawn_inputs(seed))
    spreads = {}
    factors = {'L0_ffn_b': 6.456}
    for name, (base, spread) in spreads.items():
        noise = np.random.default_rng([zlib.crc32(name.encode()), seed]).standard_normal(out[name].shape)
        drawn = base * np.exp(spread * noise) if base else spread * noise
        out[name] = jnp.asarray(drawn.astype(out[name].dtype))
    for name, factor in factors.items():
        out[name] = (out[name] * factor).astype(out[name].dtype)
    return out
```

```python
from contextlib import ExitStack

import concourse.bass as bass
from concourse import mybir

F32 = mybir.dt.float32
BF16 = mybir.dt.bfloat16
ALU = mybir.AluOpType
ACT = mybir.ActivationFunctionType
AX = mybir.AxisListType

P = 128
BATCH, SEQ, DM = 4, 2048, 256
HEADS, HD = 16, 16
KC = DM // P
CH = 512
NB = CH // P
NCH = BATCH * SEQ // CH
CPB = SEQ // CH
QH = 4
QUADS = HEADS // QH
ITERS = BATCH * QUADS
STRIP = 32
SPLITS = 3
PAIRS = [(0, 0), (0, 1), (0, 2), (1, 0), (1, 1), (2, 0)]
KROWS = len(PAIRS) * HD
EPS = 1e-5
SCALE = HD ** -0.5
X_INT = -100.0
SLOPE = -1.0 / 100.0
BOUND = 0.99 * -X_INT / SCALE
DIVISOR = 1000.0
AHEAD, BEHIND = CPB + 1, CPB

S_BUFS, R_BUFS, P_BUFS, LAG = 2, 4, 2, 2

TILES = []
for ci in range(CPB):
    c = CPB - 1 - ci
    TILES += [(ci, c, NB * c + m, P * m) for m in range(NB)]
    TILES += [(ci, c, j, 0) for j in range(NB * c - 1, -1, -1)]
NT = len(TILES)
NHALF = 2 * NT
DIAG = [t for t, (ci, c, j, off) in enumerate(TILES) if j >= NB * c]
FIRST = [next(t for t, x in enumerate(TILES) if x[0] == ci) for ci in range(CPB)]
LAST = [max(t for t, x in enumerate(TILES) if x[0] == ci) for ci in range(CPB)]

JOBS = [
    ("B", "qk", 0, 0, "act"), ("B", "qk", 1, 4, "act"), ("B", "qk", 2, 8, "act"), ("B", "qk", 3, 12, "act"),
    ("C", "proj", 0, 16, "dve"), ("C", "proj", 1, 20, "dve"),
    ("A", "z1T", 0, 24, "act"), ("A", "z1T", 1, 25, "act"),
    ("B", "v", 0, 27, "act"), ("B", "v", 1, 31, "act"),
    ("A", "ffn", 0, 35, "dve"), ("A", "ffn", 1, 39, "dve"),
    ("C", "z3T", 0, 43, "act"), ("C", "z3T", 1, 44, "act"),
    ("B", "T", 0, 46, "act"), ("C", "out", 0, 47, "dve"),
    ("B", "T", 1, 51, "act"), ("C", "out", 1, 52, "dve"),
    ("B", "T", 2, 56, "act"), ("B", "state", 0, 57, "dve"),
    ("B", "T", 3, 60, "act"), ("B", "state", 1, 61, "dve"),
    ("A", "z2T", 0, 65, "act"), ("A", "z2T", 1, 66, "act"),
    ("B", "state", 2, 68, "dve"), ("B", "state", 3, 71, "dve"),
]
PIECES = {"z1T": 1, "z2T": 1, "z3T": 1, "T": 1, "state": 3, "ffn": 4, "out": 4, "proj": 4, "qk": 4, "v": 4}
LN_AT = {"ln1": (10, 13, 14, 15), "ln3": (26, 29, 30, 31), "ln2": (46, 49, 50, 51)}


def empty_at(kind, start):
    return start + PIECES[kind] + 1


class Counts:

    def __init__(self, **stages):
        self.jobs = [x for x in JOBS if not isinstance(stages[x[0]], tuple)]
        self.before = {k: v[1] if isinstance(v, tuple) else v for k, v in stages.items()}

    def base(self, by=None):
        per = {stage: sum(x[0] == stage and by in (None, x[4]) for x in JOBS) for stage in "ABC"}
        return sum(self.before[stage] * per[stage] for stage in "ABC")

    def local(self, kind, i, by=None):
        n = 0
        for _, k, x, _, who in self.jobs:
            n += by in (None, who)
            if (k, x) == (kind, i):
                return n
        raise KeyError(kind)

    def made(self, kind, i):
        return self.base() + self.local(kind, i)

    def emptied(self, kind, i):
        who = next(x[4] for x in self.jobs if (x[1], x[2]) == (kind, i))
        return who, self.base(who) + self.local(kind, i, who)


def build(nc, x_in, w_attn, w_proj, ffn_w, ffn_b, ffn_v, ffn_c, out):
    ctx = ExitStack()
    with ctx:
        def sb(name, shape, dt=F32):
            return ctx.enter_context(nc.sbuf_tensor(name, shape, dt))

        def ps(name, shape, dt=F32):
            return ctx.enter_context(nc.psum_tensor(name, shape, dt))

        def sem(name):
            return ctx.enter_context(nc.semaphore(name))

        x_d = x_in.rearrange("b t d -> (b t) d")
        out_d = out.rearrange("b t d -> (b t) d")
        x1_d = nc.dram_tensor("x1_scratch", [NCH * CH, DM], F32, kind="Internal").ap()
        part_d = nc.dram_tensor("part_scratch", [NCH, P // HD, 2, KC, SPLITS, HD, CH], BF16, kind="Internal").ap()
        qT_d = nc.dram_tensor("qT_scratch", [NCH, DM, CH], F32, kind="Internal").ap()
        v_d = nc.dram_tensor("v_scratch", [NCH * CH, HEADS * STRIP], F32, kind="Internal").ap()
        st_d = nc.dram_tensor("state_scratch", [BATCH, CPB * NB + 1, QH * HD + 1, HEADS * STRIP], F32, kind="Internal").ap()
        y_d = nc.dram_tensor("y_scratch", [DM, NCH * CH], F32, kind="Internal").ap()

        ident = sb("ident", [P, P])
        ones = sb("ones", [P, 1])
        vr_in = sb("vr_in", [P, KC, 32])
        c_in = sb("c_in", [P, KC, 32])
        vrT = sb("vrT", [32, DM])
        cT = sb("cT", [32, DM])
        w_ffn = sb("w_ffn", [P, KC, DM])
        w_qkv = sb("w_qkv", [P, KC, 3 * DM])
        w_out = sb("w_out", [P, KC, DM])
        bias = sb("bias", [P, DM])
        bias_half = sb("bias_half", [P, DM])
        smask = sb("smask", [QH * HD + 1, HEADS * STRIP])
        qs = sb("qs", [KROWS, QH, SEQ], BF16)
        ks = sb("ks", [KROWS, QH, SEQ], BF16)
        vt = sb("vt", [P, SEQ // P, QH * STRIP])
        qT = sb("qT", [QH * HD + 1, SEQ])
        st = sb("st", [QH * HD + 1, SEQ // P, QH * STRIP])
        relu = [sb(f"relu{i}", [P, 2, CH]) for i in range(R_BUFS)]
        poly = [sb(f"poly{i}", [P, 2, CH]) for i in range(2 * P_BUFS)]
        lin = [sb(f"lin{i}", [P, QH, P]) for i in range(2)]
        y_sb = [sb(f"y_sb{i}", [P, CH]) for i in range(2)]
        x_sb = sb("x_sb", [P, NB, DM])
        x1 = sb("x1", [P, NB, DM])
        z = sb("z", [P, NB, DM])
        zT = sb("zT", [P, KC, CH])
        z2T = sb("z2T", [P, KC, CH])
        qk_sb = sb("qk_sb", [P, NB, 2 * DM])
        v_sb = sb("v_sb", [P, NB, HEADS, STRIP])
        qkT = sb("qkT", [P, 4, CH])
        parts = sb("parts", [P, 4, SPLITS, CH], BF16)
        rest = sb("rest", [P, CH])
        st_new = sb("st_new", [QH * HD + 1, NB + 1, HEADS * STRIP])
        st_add = [sb(f"st_add{i}", [QH * HD + 1, HEADS * STRIP]) for i in range(2)]
        y_c = sb("y_c", [P, KC, CH])
        x1c = sb("x1c", [P, NB, DM])
        x2 = sb("x2", [P, NB, DM])
        z3 = sb("z3", [P, NB, DM])
        z3T = sb("z3T", [P, KC, CH])
        w_in = z3[:, 0:KC, :]
        LNS = ("ln1", "ln2", "ln3")
        bnst = {k: sb(f"bnst_{k}", [P, NB, 6]) for k in LNS}
        mv = {k: sb(f"mv_{k}", [P, NB, 2]) for k in LNS}
        var = {k: sb(f"var_{k}", [P, NB]) for k in LNS}
        sd = {k: sb(f"sd_{k}", [P, NB]) for k in LNS}
        rstd = {k: sb(f"rstd_{k}", [P, NB]) for k in LNS}
        shift = {k: sb(f"shift_{k}", [P, NB]) for k in LNS}

        qk_max = sb("qk_max", [P, NCH, 2 * KC])
        qk_top = sb("qk_top", [P, 2 * KC])
        qk_prod = sb("qk_prod", [P, KC])
        head_bound = sb("head_bound", [1, HEADS])
        bound = sb("bound", [1, 1])
        no_low = sb("no_low", [1, 1], mybir.dt.int32)

        score = [ps(f"score{i}", [P, 2, CH]) for i in range(S_BUFS)]
        y_ps = [ps(f"y_ps{i}", [P, CH]) for i in range(2)]
        bank = [ps(f"bank{i}", [P, CH]) for i in range(2)]

        w_loaded = sem("w_loaded")
        const_ready = sem("const_ready")
        setup_pe = sem("setup_pe")
        setup_act = sem("setup_act")
        st_zero = sem("st_zero")
        job_done = sem("job_done")
        emptied = {"act": sem("emptied_act"), "dve": sem("emptied_dve")}
        x_loaded = sem("x_loaded")
        st_loaded = sem("st_loaded")
        x1_stored = sem("x1_stored")
        v_stored = sem("v_stored")
        qT_stored = sem("qT_stored")
        parts_stored = sem("parts_stored")
        st_stored = sem("st_stored")
        c_loaded = sem("c_loaded")
        out_stored = sem("out_stored")
        xb_ready = sem("xb_ready")
        x2b_ready = sem("x2b_ready")
        stats_done = {k: sem(f"stats_{k}") for k in LNS}
        aggr_done = {k: sem(f"aggr_{k}") for k in LNS}
        var_done = {k: sem(f"var_done_{k}") for k in LNS}
        sd_done = {k: sem(f"sd_done_{k}") for k in LNS}
        rstd_done = {k: sem(f"rstd_done_{k}") for k in LNS}
        norm_ready = {k: sem(f"norm_ready_{k}") for k in LNS}
        z_ready = {k: sem(f"z_ready_{k}") for k in LNS}
        split_step = sem("split_step")
        st_added = sem("st_added")
        kv_loaded = [sem(f"kv_loaded{c}") for c in range(CPB)]
        qk_done = sem("qk_done")
        relu_done = sem("relu_done")
        masked = sem("masked")
        poly_done = sem("poly_done")
        pv_done = sem("pv_done")
        y_copied = sem("y_copied")
        y_stored = [sem(f"y_stored{i}") for i in range(2)]

        bounded = sem("bounded")
        bound_step = sem("bound_step")
        bound_ready = sem("bound_ready")
        bound_transposed = sem("bound_transposed")
        low_loaded = sem("low_loaded")
        low_scored = sem("low_scored")
        low_line = sem("low_line")
        low_ready = sem("low_ready")
        low_masked = sem("low_masked")
        low_summed = sem("low_summed")
        low_y_loaded = sem("low_y_loaded")
        low_added = sem("low_added")
        low_stored = sem("low_stored")

        CONSTS = 11
        waits_met = {e.engine: sem(f"waits_met_{i}") for i, e in enumerate((nc.gpsimd, nc.sync, nc.vector))}
        KV_LOADS = SPLITS + len(PAIRS) + 3

        PART_STORES = P // HD

        def phases(eng, body, first=lambda: None, prefetching=False):
            none, all_ = ("done", 0), ("done", NCH)
            body(None, 0, None, None, Counts(A=0, B=none, C=none))
            with eng.Fori(0, AHEAD) as b:
                body(None, b + 1, b, None, Counts(A=b + 1, B=b, C=none))
            first()
            with eng.Fori(0, BEHIND) as n:
                body(n, n + AHEAD + 1, n + AHEAD, None, Counts(A=n + AHEAD + 1, B=n + AHEAD, C=none))
            with eng.Fori(BEHIND, NCH - AHEAD - 1) as n:
                body(n, n + AHEAD + 1, n + AHEAD, n - BEHIND, Counts(A=n + AHEAD + 1, B=n + AHEAD, C=n - BEHIND))
            n = NCH - AHEAD - 1
            body(n, None, NCH - 1, n - BEHIND, Counts(A=all_, B=NCH - 1, C=n - BEHIND))
            with eng.Fori(NCH - AHEAD, ITERS - prefetching) as n:
                body(n, None, None, n - BEHIND, Counts(A=all_, B=all_, C=n - BEHIND))
            if prefetching:
                n = ITERS - 1
                body(n, None, None, n - BEHIND, Counts(A=all_, B=all_, C=n - BEHIND), prefetch=False)
            with eng.Fori(ITERS, ITERS + BEHIND) as n:
                body(None, None, None, n - BEHIND, Counts(A=all_, B=all_, C=n - BEHIND))

        def lows(eng, correct, body):
            eng.wait_ge(bound_ready, 4)
            fine = eng.value_load(no_low[0:1, 0:1], min_val=0, max_val=1)
            with eng.If(fine < 1):
                with eng.Fori(0, ITERS) as n:
                    correct(n)
                with eng.Fori(NCH, 2 * NCH) as c:
                    body(None, None, None, c, Counts(A=("done", NCH), B=("done", NCH), C=c), again=True)
                if eng == nc.sync:
                    eng.wait_ge(out_stored, 16 * 2 * NCH)

        def wait_alone(eng, sem, value):
            eng.wait_ge(sem, value)
            eng.sem_inc(waits_met[eng.engine], 1)

        def wait_emptied(eng, counts, kind, i):
            who, value = counts.emptied(kind, i)
            wait_alone(eng, emptied[who], value) if eng in (nc.gpsimd, nc.sync) else eng.wait_ge(emptied[who], value)

        block = ctx.enter_context(nc.Block())

        @block.sync
        def _(sp):
            sp.dma_start(w_in[:], ffn_w.rearrange("(k p) d -> p k d", p=P)).then_inc(w_loaded, 16)
            sp.dma_start(vr_in[:], ffn_v.rearrange("(k p) r -> p k r", p=P)).then_inc(w_loaded, 16)
            sp.dma_start(c_in[:], ffn_c.rearrange("(k p) r -> p k r", p=P)).then_inc(w_loaded, 16)
            sp.dma_start(w_qkv[:], w_attn.rearrange("(k p) n -> p k n", p=P)).then_inc(w_loaded, 16)
            sp.dma_start(w_out[:], w_proj.rearrange("(k p) n -> p k n", p=P)).then_inc(w_loaded, 16)
            sp.dma_start(bias[:], ffn_b.rearrange("(a n) -> a n", a=1).broadcast_to([P, DM])).then_inc(w_loaded, 16)
            sp.wait_ge(const_ready, 5)
            for b in range(BATCH):
                sp.dma_start(st_d[b, 0], st_new[:, 0, :]).then_inc(st_zero, 16)
            sp.wait_ge(st_zero, 16 * BATCH)

            def load_kv(n, c, where=None):
                b, g = n // QUADS, n % QUADS
                a = b * CPB + c
                cols = slice(CH * c, CH * c + CH)
                where = kv_loaded[c] if where is None else where

                row = 0
                for q_part in range(SPLITS):
                    reps = sum(q == q_part for q, _ in PAIRS)
                    dst = slice(row, row + reps * HD)
                    src = part_d[bass.ds(a, 1), bass.ds((g % 2) * QH, QH), :, bass.ds(g // 2, 1)]
                    sp.dma_start(ks[dst, :, cols], src[:, :, 1, :, 0:reps].rearrange("o h g s d t -> (o g s d) h t")).then_inc(where, 16)
                    for r in range(reps):
                        sp.dma_start(qs[row + r * HD:row + r * HD + HD, :, cols],
                                     src[:, :, 0, :, q_part].rearrange("o h g d t -> (o g d) h t")).then_inc(where, 16)
                    row += reps * HD
                sp.dma_start(vt[:, NB * c:NB * c + NB, :],
                             v_d[bass.ds(a * CH, CH), bass.ds(g * QH * STRIP, QH * STRIP)]
                             .rearrange("(i p) n -> p i n", p=P)).then_inc(where, 16)
                sp.dma_start(qT[0:QH * HD, cols],
                             qT_d[bass.ds(a, 1), bass.ds(g * QH * HD, QH * HD), :]
                             .rearrange("o r t -> (o r) t")).then_inc(where, 16)
                sp.dma_start(st[:, NB * c:NB * c + NB, :],
                             st_d[bass.ds(b, 1), NB * c:NB * c + NB, :, bass.ds(g * QH * STRIP, QH * STRIP)]
                             .rearrange("o m r n -> (o r) m n")).then_inc(where, 16)

            def body(n, a, b, cc, counts, prefetch=True, again=False):
                if cc is not None:
                    tok_c = (cc - NCH) * CH if again else cc * CH
                for t in range(NHALF + 1):
                    if a is not None and t == 0:
                        wait_alone(sp, emptied["dve"], counts.base("dve"))
                        sp.dma_start(x_sb[:], x_d[bass.ds(a * CH, CH), :].rearrange("(i p) d -> p i d", p=P)).then_inc(x_loaded, 16)
                    if cc is not None and t == 0:
                        for i in range(2):
                            wait_alone(sp, y_stored[i], (cc + BEHIND if n is not None else ITERS) * (16 * QH * CPB // 2))
                        sp.dma_start(y_c[:], y_d[:, bass.ds(tok_c, CH)].rearrange("(k p) t -> p k t", p=P)).then_inc(c_loaded, 16)
                        sp.dma_start(x1c[:], x1_d[bass.ds(tok_c, CH), :].rearrange("(i p) d -> p i d", p=P)).then_inc(c_loaded, 16)
                    if a is not None and t == 46:
                        wait_emptied(sp, counts, "ffn", 1)
                        sp.dma_start(x1_d[bass.ds(a * CH, CH), :].rearrange("(i p) d -> p i d", p=P), x1[:]).then_inc(x1_stored, 16)
                    if b is not None and t == 20:
                        wait_alone(sp, st_stored, b * 16)
                        sp.dma_start(st_new[:, 0, :], st_d[bass.ds(b // CPB, 1), bass.ds((b % CPB) * NB, 1), :, :]
                                     .rearrange("o m r n -> (o m r) n")).then_inc(st_loaded, 16)
                    if b is not None and t == 36:
                        wait_emptied(sp, counts, "v", 1)
                        sp.dma_start(v_d[bass.ds(b * CH, CH), :].rearrange("(i p) n -> p i n", p=P),
                                     v_sb[:].rearrange("p i h s -> p i (h s)")).then_inc(v_stored, 16)
                    if b is not None and t == 54:
                        wait_emptied(sp, counts, "T", 1)
                        sp.dma_start(qT_d[bass.ds(b, 1), :, :].rearrange("o (g p) t -> (o p) g t", p=P),
                                     qkT[:, 0:2, :]).then_inc(qT_stored, 16)
                    if cc is not None and t == 58:
                        wait_emptied(sp, counts, "out", 1)
                        sp.dma_start(out_d[bass.ds(tok_c, CH), :].rearrange("(i p) d -> p i d", p=P), x2[:]).then_inc(out_stored, 16)
                    if b is not None and t == 70:
                        wait_alone(sp, split_step, (b + 1) * 12)
                        for h in range(P // HD):
                            sp.dma_start(part_d[bass.ds(b, 1), h].rearrange("o w g s d t -> (o d) (w g s) t"),
                                         parts[HD * h:HD * h + HD].rearrange("p g s t -> p (g s) t")).then_inc(parts_stored, 16)
                    if b is not None and t == NHALF:
                        wait_alone(sp, st_added, (b + 1) * NB)
                        sp.dma_start(st_d[bass.ds(b // CPB, 1), bass.ds((b % CPB) * NB + 1, NB), :, :]
                                     .rearrange("o m r n -> (o r) m n"), st_new[:, 1:NB + 1, :]).then_inc(st_stored, 16)
                    if n is not None:
                        for ci in range(CPB):
                            if t == min(2 * (LAST[ci] + LAG + 1), NHALF):
                                wait_alone(sp, y_copied, n * CPB + ci + 1)
                                for h in range(QH):
                                    sp.dma_start(y_d[bass.ds((n % QUADS) * QH * HD + h * HD, HD),
                                                     bass.ds((n // QUADS) * SEQ + (CPB - 1 - ci) * CH, CH)],
                                                 y_sb[ci % 2][STRIP * h:STRIP * h + HD, :]).then_inc(y_stored[ci % 2], 16)
                                if ci == 0:
                                    chunks = b if b is not None else NCH
                                    all_stored(chunks)
                                if prefetch:
                                    load_kv(n + 1, CPB - 1 - ci)

            def all_stored(chunks):
                wait_alone(sp, v_stored, chunks * 16)
                wait_alone(sp, qT_stored, chunks * 16)
                wait_alone(sp, parts_stored, chunks * (16 * PART_STORES))
                wait_alone(sp, st_stored, chunks * 16)

            def first():
                all_stored(AHEAD)
                for ci in range(CPB):
                    load_kv(0, CPB - 1 - ci)

            phases(sp, body, first, prefetching=True)
            sp.wait_ge(out_stored, 16 * NCH)
            sp.wait_ge(x1_stored, 16 * NCH)
            for i in range(2):
                sp.wait_ge(y_stored[i], ITERS * (16 * QH * CPB // 2))

            def correct(n):
                if True:
                    for c in range(CPB):
                        load_kv(n, c, low_loaded)
                for ci in range(CPB):
                    strips = [(y_d[bass.ds((n % QUADS) * QH * HD + h * HD, HD), bass.ds((n // QUADS) * SEQ + (CPB - 1 - ci) * CH, CH)],
                               slice(STRIP * h, STRIP * h + HD)) for h in range(QH)]
                    for dram, rows in strips:
                        sp.dma_start(y_sb[0][rows, :], dram).then_inc(low_y_loaded, 16)
                    wait_alone(sp, low_added, n * CPB + (ci + 1))
                    for dram, rows in strips:
                        sp.dma_start(dram, y_sb[1][rows, :]).then_inc(low_stored, 16)
                    wait_alone(sp, low_stored, (n * CPB + (ci + 1)) * (16 * QH))

            lows(sp, correct, body)

        @block.gpsimd
        def _(pool):
            pool.memset(ident[:], 0.0).then_inc(const_ready, 1)
            pool.memset(smask[:], SLOPE * SCALE).then_inc(const_ready, 1)
            pool.memset(st_new[:], 0.0).then_inc(const_ready, 1)
            pool.memset(v_sb[:], 0.0).then_inc(const_ready, 1)
            pool.memset(ones[:], 1.0).then_inc(const_ready, 1)
            pool.memset(qT[:], 1.0).then_inc(const_ready, 1)
            pool.wait_ge(const_ready, 6)
            pool.affine_select(out=ident[:], in_=ident[:], compare_op=ALU.not_equal, fill=1.0, base=0,
                               pattern=[[-1, P]], channel_multiplier=1).then_inc(const_ready, 1)
            rows = smask[0:QH * HD, :]
            pool.affine_select(out=rows, in_=rows, compare_op=ALU.is_ge, fill=0.0, base=0,
                               pattern=[[0, QUADS], [-HD, QH], [0, STRIP]], channel_multiplier=1).then_inc(const_ready, 1)
            pool.wait_ge(const_ready, 8)
            pool.affine_select(out=rows, in_=rows, compare_op=ALU.is_ge, fill=0.0, base=HD - 1,
                               pattern=[[0, QUADS], [HD, QH], [0, STRIP]], channel_multiplier=-1).then_inc(const_ready, 1)
            pool.memset(smask[QH * HD:QH * HD + 1, :], 1.0).then_inc(const_ready, 1)
            pool.wait_ge(w_loaded, 16 * 6)
            pool.wait_ge(const_ready, 10)
            pool.tensor_scalar(bias_half[:], bias[:], 0.5, 0.0, ALU.mult, ALU.add).then_inc(const_ready, 1)
            pool.wait_ge(const_ready, CONSTS)

            def normalise(k, src, dst, value, last_read=None):
                wait_alone(pool, norm_ready[k], value)
                for i in range(NB):
                    ins = pool.tensor_scalar(dst[:, i, :], src[:, i, :], rstd[k][:, i:i + 1], shift[k][:, i:i + 1],
                                             ALU.mult, ALU.add)
                ins.then_inc(z_ready[k], 1)

            def add_bias(dst, src, ready):
                pool.tensor_tensor(dst[:], src[:], bias_half[:, None, :].broadcast_to([P, NB, DM]), ALU.add).then_inc(ready, 1)

            def body(n, a, b, cc, counts, again=False):
                for t in range(NHALF + 1):
                    if n is not None and t // 2 in DIAG:
                        m = DIAG.index(t // 2)
                        off = TILES[t // 2][3]
                        wait_alone(pool, relu_done, n * NHALF + (S_BUFS + t + 1))
                        for buf in (relu[t % R_BUFS][:, :, off:off + P], lin[m % 2][:, 2 * (t % 2):2 * (t % 2) + 2, :]):
                            pool.affine_select(out=buf, in_=buf, compare_op=ALU.is_ge, fill=0.0, base=0,
                                               pattern=[[0, 2], [1, P]], channel_multiplier=-1).then_inc(masked, 1)
                    if a is not None:
                        if t == LN_AT["ln1"][3]:
                            normalise("ln1", x_sb, z, a + 1)
                            wait_alone(pool, z_ready["ln1"], a + 1)
                            add_bias(x_sb, x_sb, xb_ready)
                        if t == LN_AT["ln2"][3]:
                            wait_alone(pool, job_done, counts.made("z1T", 1))
                            normalise("ln2", x1, z, a + 1)
                    if cc is not None and t == LN_AT["ln3"][3]:
                        normalise("ln3", x2, z3, cc + 1)
                        wait_alone(pool, z_ready["ln3"], cc + 1)
                        add_bias(x2, x2, x2b_ready)
                    for _, kind, i, start, _ in counts.jobs:
                        if kind == "T" and t == empty_at(kind, start) + 1:
                            wait_emptied(pool, counts, "T", i)
                            if i == 0:
                                wait_alone(pool, parts_stored, b * (16 * PART_STORES))
                            wait_alone(pool, split_step, b * 12 + 3 * i)
                            pool.tensor_tensor(rest[:], qkT[:, i, :], parts[:, i, 0, :], ALU.subtract).then_inc(split_step, 1)
                            wait_alone(pool, split_step, b * 12 + 3 * i + 1)
                            pool.tensor_copy(parts[:, i, 1, :], rest[:]).then_inc(split_step, 1)
                            wait_alone(pool, split_step, b * 12 + 3 * i + 2)
                            pool.tensor_tensor(parts[:, i, 2, :], rest[:], parts[:, i, 1, :], ALU.subtract).then_inc(split_step, 1)
                        if kind == "state" and t == min(empty_at(kind, start) + 1, NHALF):
                            if i == 0:
                                wait_alone(pool, st_loaded, (b + 1) * 16)
                            else:
                                wait_alone(pool, st_added, b * NB + i)
                            wait_emptied(pool, counts, "state", i)
                            pool.tensor_tensor(st_new[:, i + 1, :], st_new[:, i, :], st_add[i % 2][:], ALU.add).then_inc(st_added, 1)

            phases(pool, body)

            def correct(n):
                for m, t in enumerate(DIAG):
                    for half in range(2):
                        off = TILES[t][3]
                        wait_alone(pool, low_ready, n * NHALF + (2 * t + half + 1))
                        buf = poly[0][:, :, off:off + P]
                        pool.affine_select(out=buf, in_=buf, compare_op=ALU.is_ge, fill=0.0, base=0,
                                           pattern=[[0, 2], [1, P]], channel_multiplier=-1).then_inc(low_masked, 1)

            lows(pool, correct, body)

        @block.scalar
        def _(act):
            act.sem_inc(relu_done, S_BUFS)
            act.wait_ge(setup_pe, 1)
            nc.scalar.activation(vrT[:], score[0][0:32, 0, 0:DM], ACT.Copy).then_inc(setup_act, 1)
            nc.scalar.activation(cT[:], score[0][0:32, 0, DM:2 * DM], ACT.Copy).then_inc(setup_act, 1)
            for k in range(KC):
                act.wait_ge(setup_pe, 2 + k)
                nc.scalar.activation(w_ffn[:, k, :], y_ps[k][:, 0:DM], ACT.Copy, scale=0.5).then_inc(setup_act, 1)
            act.wait_ge(const_ready, CONSTS)

            def root(k, value):
                act.wait_ge(var_done[k], value)
                nc.scalar.activation(sd[k][:], var[k][:], ACT.Sqrt).then_inc(sd_done[k], 1)

            def empty(b, kind, i, src):
                done = emptied["act"]
                if kind in ("z1T", "z2T", "z3T"):
                    dst = {"z1T": zT, "z2T": z2T, "z3T": z3T}[kind]
                    nc.scalar.activation(dst[:, i, :], src[:], ACT.Copy).then_inc(done, 1)
                if kind == "qk":
                    nc.scalar.activation(qk_sb[:, i, :], src[:], ACT.Copy).then_inc(done, 1)
                if kind == "v":
                    if i == 0:
                        act.wait_ge(v_stored, b * 16)
                    nc.scalar.activation(v_sb[:, 2 * i:2 * i + 2, :, 0:HD], src[:].rearrange("p (b h d) -> p b h d", b=2, h=HEADS),
                                         ACT.Copy).then_inc(done, 1)
                if kind == "T":
                    if i == 0:
                        act.wait_ge(qT_stored, b * 16)
                        act.wait_ge(parts_stored, b * (16 * PART_STORES))
                        act.wait_ge(bounded, b)
                    nc.scalar.activation(qkT[:, i, :], src[:], ACT.Copy)
                    nc.scalar.activation(parts[:, i, 0, :], src[:], ACT.Copy).then_inc(done, 1)

            def body(n, a, b, cc, counts, again=False):
                for t in range(NHALF + 2 * LAG + 2):
                    for k, (_, kind, i, start, who) in enumerate(counts.jobs):
                        if who == "act" and t == empty_at(kind, start):
                            act.wait_ge(job_done, counts.made(kind, i))
                            empty(b, kind, i, bank[k % 2])
                    if n is not None and t < NHALF:
                        ci, c, j, off = TILES[t // 2]
                        act.wait_ge(qk_done, n * NHALF + t + 1)
                        if t // 2 in DIAG:
                            act.wait_ge(pv_done, n * NT + t // 2 + 1)
                            nc.scalar.activation(lin[DIAG.index(t // 2) % 2][:, 2 * (t % 2):2 * (t % 2) + 2, :],
                                                 score[t % S_BUFS][:, :, off:off + P], ACT.Copy,
                                                 scale=SLOPE * SCALE, bias=1.0)
                        act.wait_ge(poly_done, n * NHALF + t + 1)
                        nc.scalar.activation(relu[t % R_BUFS][:, :, off:CH], score[t % S_BUFS][:, :, off:CH], ACT.Relu,
                                             scale=SCALE).then_inc(relu_done, 1)
                    if n is not None:
                        for ci in range(CPB):
                            if t == 2 * (LAST[ci] + LAG) + 2:
                                act.wait_ge(pv_done, n * NT + (P_BUFS + LAST[ci] + 1))
                                act.wait_ge(y_stored[ci % 2], n * (16 * QH * CPB // 2) + (ci // 2) * 16 * QH)
                                nc.scalar.activation(y_sb[ci % 2][:], y_ps[ci % 2][:], ACT.Copy).then_inc(y_copied, 1)
                    if a is not None and t == LN_AT["ln1"][1]:
                        root("ln1", a + 1)
                    if a is not None and t == LN_AT["ln2"][1]:
                        root("ln2", a + 1)
                    if cc is not None and t == LN_AT["ln3"][1]:
                        root("ln3", cc + 1)

            phases(act, body)
            lows(act, lambda n: None, body)

        @block.vector
        def _(dve):
            dve.sem_inc(poly_done, R_BUFS)
            dve.wait_ge(const_ready, CONSTS)

            def stats(k, src, value):
                for i in range(NB):
                    nc.vector.bn_stats(bnst[k][:, i, :], src[:, i, :]).then_inc(stats_done[k], 1)
                wait_alone(dve, stats_done[k], (value + 1) * NB)
                for i in range(NB):
                    nc.vector.bn_aggr(mv[k][:, i, :], bnst[k][:, i, :]).then_inc(aggr_done[k], 1)
                dve.wait_ge(aggr_done[k], (value + 1) * NB)
                nc.vector.tensor_scalar(var[k][:], mv[k][:, :, 1], EPS, None, ALU.add).then_inc(var_done[k], 1)

            def scales(k, value):
                dve.wait_ge(sd_done[k], value + 1)
                nc.vector.reciprocal(rstd[k][:], sd[k][:]).then_inc(rstd_done[k], 1)
                dve.wait_ge(rstd_done[k], value + 1)
                nc.vector.scalar_tensor_tensor(shift[k][:], mv[k][:, :, 0], -1.0, rstd[k][:], ALU.mult, ALU.mult).then_inc(norm_ready[k], 1)

            def empty(a, b, cc, kind, i, src):
                done = emptied["dve"]
                two = src[:].rearrange("p (b d) -> p b d", b=2)
                if kind == "ffn":
                    if i == 0:
                        dve.wait_ge(xb_ready, a + 1)
                        dve.wait_ge(x1_stored, a * 16)
                    nc.vector.tensor_tensor(x1[:, 2 * i:2 * i + 2, :], two, x_sb[:, 2 * i:2 * i + 2, :], ALU.add).then_inc(done, 1)
                if kind == "proj":
                    if i == 0:
                        dve.wait_ge(c_loaded, (cc + 1) * 32)
                        dve.wait_ge(out_stored, cc * 16)
                    nc.vector.scalar_tensor_tensor(x2[:, 2 * i:2 * i + 2, :], two, 1.0 / DIVISOR, x1c[:, 2 * i:2 * i + 2, :],
                                                   ALU.mult, ALU.add).then_inc(done, 1)
                if kind == "out":
                    if i == 0:
                        dve.wait_ge(x2b_ready, cc + 1)
                    nc.vector.tensor_tensor(x2[:, 2 * i:2 * i + 2, :], two, x2[:, 2 * i:2 * i + 2, :], ALU.add).then_inc(done, 1)
                if kind == "state":
                    if i >= 2:
                        dve.wait_ge(st_added, b * NB + i - 1)
                    nc.vector.tensor_tensor(st_add[i % 2][:], src[0:QH * HD + 1, :], smask[:], ALU.mult).then_inc(done, 1)

            def body(n, a, b, cc, counts, again=False):
                for t in range(NHALF + 1):
                    for k, (_, kind, i, start, who) in enumerate(counts.jobs):
                        if who == "dve" and t == empty_at(kind, start):
                            dve.wait_ge(job_done, counts.made(kind, i))
                            empty(a, b, cc, kind, i, bank[k % 2])
                    if n is not None and t < NHALF:
                        ci, c, j, off = TILES[t // 2]
                        if t // 2 in DIAG:
                            dve.wait_ge(masked, n * 4 * len(DIAG) + 4 * DIAG.index(t // 2) + 2 * (t % 2) + 2)
                        else:
                            dve.wait_ge(relu_done, n * NHALF + (S_BUFS + t + 1))
                        if t % 2 == 0:
                            dve.wait_ge(pv_done, n * NT + t // 2 + 1)
                        r = relu[t % R_BUFS][:, :, off:CH]
                        nc.vector.scalar_tensor_tensor(poly[t % (2 * P_BUFS)][:, :, off:CH], r, -SLOPE, r,
                                                       ALU.add, ALU.mult).then_inc(poly_done, 1)
                    if b is not None and t == 64:
                        wait_emptied(dve, counts, "T", 3)
                        nc.vector.tensor_reduce(qk_max[:, bass.ds(b, 1), :].rearrange("p c g -> p (c g)"), qkT[:], AX.X, ALU.max,
                                                apply_absolute_value=True).then_inc(bounded, 1)
                    if a is not None:
                        if t == LN_AT["ln1"][0]:
                            dve.wait_ge(x_loaded, (a + 1) * 16)
                            stats("ln1", x_sb, a)
                        if t == LN_AT["ln1"][2]:
                            scales("ln1", a)
                        if t == LN_AT["ln2"][0]:
                            wait_emptied(dve, counts, "ffn", 1)
                            stats("ln2", x1, a)
                        if t == LN_AT["ln2"][2]:
                            scales("ln2", a)
                    if cc is not None:
                        if t == LN_AT["ln3"][0]:
                            wait_emptied(dve, counts, "proj", 1)
                            stats("ln3", x2, cc)
                        if t == LN_AT["ln3"][2]:
                            scales("ln3", cc)

            phases(dve, body)

            dve.wait_ge(bounded, NCH)
            nc.vector.tensor_reduce(qk_top[:], qk_max[:].rearrange("p c g -> p g c"), AX.X, ALU.max).then_inc(bound_ready, 1)
            dve.wait_ge(bound_ready, 1)
            nc.vector.tensor_tensor(qk_prod[:], qk_top[:, 0:KC], qk_top[:, KC:2 * KC], ALU.mult).then_inc(bound_step, 1)
            dve.wait_ge(bound_transposed, 1)
            nc.vector.tensor_reduce(head_bound[:], bank[0][0:1, 0:DM].rearrange("p (h d) -> p h d", h=HEADS), AX.X, ALU.add).then_inc(bound_ready, 1)
            dve.wait_ge(bound_ready, 2)
            nc.vector.tensor_reduce(bound[:], head_bound[:], AX.X, ALU.max).then_inc(bound_ready, 1)
            dve.wait_ge(bound_ready, 3)
            nc.vector.tensor_scalar(no_low[:], bound[:], BOUND, None, ALU.is_lt).then_inc(bound_ready, 1)

            def correct(n):
                for h in range(NHALF):
                    ci, c, j, off = TILES[h // 2]
                    s = score[0][:, :, off:CH]
                    dve.wait_ge(low_scored, n * NHALF + (h + 1))
                    nc.vector.tensor_scalar(relu[0][:, :, off:CH], s, -SLOPE * SCALE, -1.0, ALU.mult, ALU.add).then_inc(low_line, 1)
                    dve.wait_ge(low_line, n * NHALF + (h + 1))
                    nc.vector.scalar_tensor_tensor(poly[0][:, :, off:CH], s, X_INT / SCALE, relu[0][:, :, off:CH],
                                                   ALU.is_lt, ALU.mult).then_inc(low_ready, 1)
                    if h == 2 * LAST[ci] + 1:
                        dve.wait_ge(low_summed, n * CPB + (ci + 1))
                        dve.wait_ge(low_y_loaded, (n * CPB + (ci + 1)) * (16 * QH))
                        nc.vector.tensor_tensor(y_sb[1][:], y_ps[0][:], y_sb[0][:], ALU.add).then_inc(low_added, 1)

            lows(dve, correct, body)

        @block.tensor
        def _(pe):
            def mm(*args, start=True, stop=True):
                return nc.tensor.matmul(*args, start=start, stop=stop, skip_group_check=True)

            pe.sem_inc(pv_done, P_BUFS)
            pe.wait_ge(const_ready, CONSTS)
            pe.wait_ge(w_loaded, 16 * 6)
            for k in range(KC):
                nc.tensor.transpose(score[0][0:32, 0, P * k:P * k + P], vr_in[:, k, :], ident[:])
                ins = nc.tensor.transpose(score[0][0:32, 0, DM + P * k:DM + P * k + P], c_in[:, k, :], ident[:])
            ins.then_inc(setup_pe, 1)
            pe.wait_ge(setup_act, 2)
            for k in range(KC):
                for o in range(KC):
                    dst = y_ps[k][:, P * o:P * o + P]
                    mm(dst, w_in[:, o, P * k:P * k + P], ident[:], start=True, stop=False)
                    ins = mm(dst, vrT[:, P * k:P * k + P], cT[:, P * o:P * o + P], start=False, stop=True)
                ins.then_inc(setup_pe, 1)
            pe.wait_ge(setup_act, 4)

            def transposes(dst, src, i):
                for blk in range(NB):
                    ins = nc.tensor.transpose(dst[:, P * blk:P * blk + P], src[:, blk, P * i:P * i + P], ident[:])
                return ins

            def job(a, b, cc, counts, k, kind, i, piece):
                dst = bank[k % 2]
                if piece == 0:
                    if k < 2:
                        for who in ("act", "dve"):
                            pe.wait_ge(emptied[who], counts.base(who))
                    else:
                        wait_emptied(pe, counts, counts.jobs[k - 2][1], counts.jobs[k - 2][2])
                first = piece == 0 and i == 0
                half = dst[:, DM * (piece // 2):DM * (piece // 2) + DM]
                kc = piece % 2
                if kind in ("z1T", "z2T", "z3T"):
                    name = {"z1T": "ln1", "z2T": "ln2", "z3T": "ln3"}[kind]
                    if first:
                        pe.wait_ge(z_ready[name], (cc if kind == "z3T" else a) + 1)
                    ins = transposes(dst, z3 if kind == "z3T" else z, i)
                if kind in ("ffn", "out", "proj", "v"):
                    if first and kind == "proj":
                        pe.wait_ge(c_loaded, (cc + 1) * 32)
                    if first and kind in ("ffn", "out"):
                        wait_emptied(pe, counts, {"ffn": "z1T", "out": "z3T"}[kind], 1)
                    src, w = {"ffn": (zT, w_ffn), "out": (z3T, w_ffn), "proj": (y_c, w_out), "v": (z2T, w_qkv[:, :, 2 * DM:])}[kind]
                    blk = 2 * i + piece // 2
                    ins = mm(half, src[:, kc, P * blk:P * blk + P], w[:, kc, :], start=kc == 0, stop=kc == KC - 1)
                if kind == "qk":
                    if first:
                        pe.wait_ge(emptied["act"], counts.base("act"))
                    cols = slice(DM * (piece // 2), DM * (piece // 2) + DM)
                    ins = mm(half, z2T[:, kc, P * i:P * i + P], w_qkv[:, kc, cols], start=kc == 0, stop=kc == KC - 1)
                if kind == "T":
                    if first:
                        wait_emptied(pe, counts, "qk", 3)
                    ins = transposes(dst, qk_sb, i)
                if kind == "state":
                    if first:
                        wait_emptied(pe, counts, "v", 1)
                    v_row = v_sb[:, i].rearrange("p h s -> p (h s)")
                    for g in range(2 * piece, min(2 * piece + 2, QUADS)):
                        k_cols = qk_sb[:, i, DM + QH * HD * g:DM + QH * HD * (g + 1)]
                        ins = mm(dst[0:QH * HD, P * g:P * g + P], k_cols, v_row[:, P * g:P * g + P])
                    if piece == 2:
                        ins = mm(dst[QH * HD:QH * HD + 1, :], ones[:], v_row)
                if piece == PIECES[kind] - 1:
                    ins.then_inc(job_done, 1)

            def score_half(n, h):
                ci, c, j, off = TILES[h // 2]
                if h % 2 == 0 and j // NB not in [x[2] // NB for x in TILES[:h // 2]]:
                    pe.wait_ge(kv_loaded[j // NB], (n + 1) * (16 * KV_LOADS))
                pe.wait_ge(relu_done, n * NHALF + h + 1)
                for u in range(2):
                    head = 2 * (h % 2) + u
                    ins = mm(score[h % S_BUFS][:, u, off:CH], ks[:, head, P * j:P * j + P],
                             qs[:, head, CH * c + off:CH * c + CH])
                ins.then_inc(qk_done, 1)

            def values(n, t):
                ci, c, j, off = TILES[t]
                y = y_ps[ci % 2]
                if t == FIRST[ci]:
                    if ci >= 2:
                        pe.wait_ge(y_copied, n * CPB + ci - 1)
                    else:
                        pe.wait_ge(y_copied, n * CPB)
                    for m in range(NB):
                        mm(y[:, P * m:P * m + P], st[:, NB * c + m, :], qT[:, CH * c + P * m:CH * c + P * m + P],
                           start=m == 0, stop=False)
                pe.wait_ge(poly_done, n * NHALF + (R_BUFS + 2 * t + 2))
                last = t == LAST[ci]
                for head in range(QH):
                    ins = mm(y[STRIP * head:STRIP * head + HD, off:CH], vt[:, j, STRIP * head:STRIP * head + HD],
                             poly[(2 * t + head // 2) % (2 * P_BUFS)][:, head % 2, off:CH], start=False, stop=last)
                if t in DIAG:
                    for head in range(QH):
                        ins = mm(y[STRIP * head:STRIP * head + HD, off:off + P], vt[:, j, STRIP * head:STRIP * head + HD],
                                 lin[DIAG.index(t) % 2][:, head, :], start=False, stop=False)
                ins.then_inc(pv_done, 1)

            def body(n, a, b, cc, counts, again=False):
                for t in range(NHALF + 2 * LAG):
                    if n is not None and t < NHALF:
                        score_half(n, t)
                    if n is not None and t % 2 and t // 2 >= LAG:
                        values(n, t // 2 - LAG)
                    for k, (_, kind, i, start, _) in enumerate(counts.jobs):
                        if 0 <= t - start < PIECES[kind]:
                            job(a, b, cc, counts, k, kind, i, t - start)

            phases(pe, body)

            pe.wait_ge(bound_step, 1)
            for who, jobs in (("act", sum(x[4] == "act" for x in JOBS)), ("dve", sum(x[4] == "dve" for x in JOBS))):
                pe.wait_ge(emptied[who], NCH * jobs)
            for g in range(KC):
                ins = nc.tensor.transpose(bank[0][0:1, P * g:P * g + P], qk_prod[:, g:g + 1], ident[:])
            ins.then_inc(bound_transposed, 1)

            def correct(n):
                pe.wait_ge(low_loaded, (n + 1) * (16 * KV_LOADS * CPB))
                for h in range(NHALF):
                    ci, c, j, off = TILES[h // 2]
                    y = y_ps[0]
                    if h == 2 * FIRST[ci]:
                        if ci == 0:
                            pe.wait_ge(low_added, n * CPB)
                        else:
                            pe.wait_ge(low_added, n * CPB + ci)
                        mm(y[:], st[:, 0, :], qT[:, 0:CH], start=True, stop=False)
                    for u in range(2):
                        head = 2 * (h % 2) + u
                        ins = mm(score[0][:, u, off:CH], ks[:, head, P * j:P * j + P], qs[:, head, CH * c + off:CH * c + CH])
                    ins.then_inc(low_scored, 1)
                    pe.wait_ge(low_ready, n * NHALF + (h + 1))
                    if h // 2 in DIAG:
                        pe.wait_ge(low_masked, n * (2 * len(DIAG)) + (2 * DIAG.index(h // 2) + h % 2 + 1))
                    for u in range(2):
                        head = 2 * (h % 2) + u
                        ins = mm(y[STRIP * head:STRIP * head + HD, off:CH], vt[:, j, STRIP * head:STRIP * head + HD],
                                 poly[0][:, u, off:CH], start=False, stop=h == 2 * LAST[ci] + 1)
                    if h == 2 * LAST[ci] + 1:
                        ins.then_inc(low_summed, 1)

            lows(pe, correct, body)


_INS = ['L0_attn_x', 'L0_attn_W_attn', 'L0_attn_W_proj', 'L0_ffn_W', 'L0_ffn_b', 'L0_ffn_V_r', 'L0_ffn_C']
_OUTS = [((BATCH, SEQ, DM), 'float32')]


def kernel(**inputs):
    import numpy as _np
    import concourse.bacc as _bacc
    from concourse import mybir as _mybir
    from concourse.bass_utils import run_bass_kernel_spmd as _run

    nc = _bacc.Bacc("TRN2", target_bir_lowering=False, num_devices=1)
    arrays, args = {}, []
    for name in _INS:
        a = _np.ascontiguousarray(inputs[name])
        arrays[f"in_{name}_dram"] = a
        args.append(nc.dram_tensor(f"in_{name}_dram", a.shape, _mybir.dt.from_np(a.dtype), kind="ExternalInput").ap())
    for i, (shape, dtype) in enumerate(_OUTS):
        dt = _mybir.dt.from_np(_np.dtype(dtype))
        args.append(nc.dram_tensor(f"out_{i}_dram", shape, dt, kind="ExternalOutput").ap())
    build(nc, *args)
    r = _run(nc, [arrays], core_ids=[0])
    return r.results[0]["out_0_dram"]
```

```python
from contextlib import ExitStack

import concourse.bass as bass
from concourse import mybir

F32 = mybir.dt.float32
BF16 = mybir.dt.bfloat16
ALU = mybir.AluOpType
ACT = mybir.ActivationFunctionType
AX = mybir.AxisListType

P = 128
BATCH, SEQ, DM = 4, 2048, 256
HEADS, HD = 16, 16
KC = DM // P
CH = 512
NB = CH // P
NCH = BATCH * SEQ // CH
CPB = SEQ // CH
QH = 4
QUADS = HEADS // QH
ITERS = BATCH * QUADS
STRIP = 32
SPLITS = 3
PAIRS = [(0, 0), (0, 1), (0, 2), (1, 0), (1, 1), (2, 0)]
KROWS = len(PAIRS) * HD
EPS = 1e-5
SCALE = HD ** -0.5
X_INT = -100.0
SLOPE = -1.0 / 100.0
BOUND = 0.99 * -X_INT / SCALE
DIVISOR = 1000.0
AHEAD, BEHIND = CPB + 1, CPB

S_BUFS, R_BUFS, P_BUFS, LAG = 2, 4, 2, 2

TILES = []
for ci in range(CPB):
    c = CPB - 1 - ci
    for m in range(NB):
        TILES.append((ci, c, NB * c + m, P * m))
        TILES += [(ci, c, NB * c - 1 - c * m - i, 0) for i in range(c)]
NT = len(TILES)
NHALF = 2 * NT
DIAG = [t for t, (ci, c, j, off) in enumerate(TILES) if j >= NB * c]
FIRST = [next(t for t, x in enumerate(TILES) if x[0] == ci) for ci in range(CPB)]
LAST = [max(t for t, x in enumerate(TILES) if x[0] == ci) for ci in range(CPB)]

JOBS = [
    ("B", "qk", 0, 0, "act"), ("B", "qk", 1, 4, "act"), ("B", "qk", 2, 8, "act"), ("B", "qk", 3, 12, "act"),
    ("C", "proj", 0, 16, "dve"), ("C", "proj", 1, 20, "dve"),
    ("A", "z1T", 0, 24, "act"), ("A", "z1T", 1, 26, "act"),
    ("A", "ffn", 0, 29, "dve"), ("A", "ffn", 1, 33, "dve"),
    ("B", "T", 0, 37, "act"), ("B", "T", 1, 39, "act"),
    ("B", "v", 0, 40, "act"), ("B", "v", 1, 44, "act"),
    ("B", "T", 2, 48, "act"), ("B", "T", 3, 50, "act"),
    ("C", "z3T", 0, 51, "act"), ("C", "z3T", 1, 53, "act"),
    ("C", "out", 0, 56, "dve"), ("C", "out", 1, 60, "dve"),
    ("B", "state", 0, 64, "dve"), ("A", "z2T", 0, 67, "act"),
    ("B", "state", 1, 69, "dve"), ("A", "z2T", 1, 72, "act"),
    ("B", "state", 2, 74, "dve"), ("B", "state", 3, 77, "dve"),
]
PIECES = {"z1T": 1, "z2T": 1, "z3T": 1, "T": 1, "state": 3, "ffn": 4, "out": 4, "proj": 4, "qk": 4, "v": 4}
LN_AT = {"ln1": 5, "ln3": 24, "ln2": 37}
AGGR, ROOT, SCALES, NORM, BIAS = NB, NB + 4, NB + 3, NB + 4, 2 * NB + 4
COPY_AT = [2 * (LAST[ci] + LAG) + 1 for ci in range(CPB)]


def empty_at(kind, start, who):
    return start + PIECES[kind] - (1 if who == "dve" else 0)


class Counts:

    def __init__(self, **stages):
        self.jobs = [x for x in JOBS if not isinstance(stages[x[0]], tuple)]
        self.before = {k: v[1] if isinstance(v, tuple) else v for k, v in stages.items()}

    def base(self, by=None):
        per = {stage: sum(x[0] == stage and by in (None, x[4]) for x in JOBS) for stage in "ABC"}
        return sum(self.before[stage] * per[stage] for stage in "ABC")

    def local(self, kind, i, by=None):
        n = 0
        for _, k, x, _, who in self.jobs:
            n += by in (None, who)
            if (k, x) == (kind, i):
                return n
        raise KeyError(kind)

    def made(self, kind, i):
        return self.base() + self.local(kind, i)

    def emptied(self, kind, i):
        who = next(x[4] for x in self.jobs if (x[1], x[2]) == (kind, i))
        return who, self.base(who) + self.local(kind, i, who)


def build(nc, x_in, w_attn, w_proj, ffn_w, ffn_b, ffn_v, ffn_c, out):
    ctx = ExitStack()
    with ctx:
        def sb(name, shape, dt=F32):
            return ctx.enter_context(nc.sbuf_tensor(name, shape, dt))

        def ps(name, shape, dt=F32):
            return ctx.enter_context(nc.psum_tensor(name, shape, dt))

        def sem(name):
            return ctx.enter_context(nc.semaphore(name))

        x_d = x_in.rearrange("b t d -> (b t) d")
        out_d = out.rearrange("b t d -> (b t) d")
        x1_d = nc.dram_tensor("x1_scratch", [NCH * CH, DM], F32, kind="Internal").ap()
        part_d = nc.dram_tensor("part_scratch", [NCH, P // HD, 2, KC, SPLITS, HD, CH], BF16, kind="Internal").ap()
        qT_d = nc.dram_tensor("qT_scratch", [NCH, DM, CH], F32, kind="Internal").ap()
        v_d = nc.dram_tensor("v_scratch", [NCH * CH, HEADS * STRIP], F32, kind="Internal").ap()
        st_d = nc.dram_tensor("state_scratch", [BATCH, CPB * NB + 1, QH * HD + 1, HEADS * STRIP], F32, kind="Internal").ap()
        y_d = nc.dram_tensor("y_scratch", [DM, NCH * CH], F32, kind="Internal").ap()

        ident = sb("ident", [P, P])
        ones = sb("ones", [P, 1])
        vr_in = sb("vr_in", [P, KC, 32])
        c_in = sb("c_in", [P, KC, 32])
        vrT = sb("vrT", [32, DM])
        cT = sb("cT", [32, DM])
        w_ffn = sb("w_ffn", [P, KC, DM])
        w_qkv = sb("w_qkv", [P, KC, 3 * DM])
        w_out = sb("w_out", [P, KC, DM])
        bias = sb("bias", [P, DM])
        bias_half = sb("bias_half", [P, DM])
        smask = sb("smask", [QH * HD + 1, HEADS * STRIP])
        qs = sb("qs", [KROWS, QH, SEQ], BF16)
        ks = sb("ks", [KROWS, QH, SEQ], BF16)
        vt = sb("vt", [P, SEQ // P, QH * STRIP])
        qT = sb("qT", [QH * HD + 1, SEQ])
        st = sb("st", [QH * HD + 1, SEQ // P, QH * STRIP])
        relu = [sb(f"relu{i}", [P, 2, CH]) for i in range(R_BUFS)]
        poly = [sb(f"poly{i}", [P, 2, CH]) for i in range(2 * P_BUFS)]
        lin = [sb(f"lin{i}", [P, QH, P]) for i in range(2)]
        y_sb = [sb(f"y_sb{i}", [P, CH]) for i in range(2)]
        x_sb = sb("x_sb", [P, NB, DM])
        x1 = sb("x1", [P, NB, DM])
        z = sb("z", [P, NB, DM])
        zT = sb("zT", [P, KC, CH])
        z2T = sb("z2T", [P, KC, CH])
        qk_sb = sb("qk_sb", [P, NB, 2 * DM])
        v_sb = sb("v_sb", [P, NB, HEADS, STRIP])
        qkT = sb("qkT", [P, 4, CH])
        parts = sb("parts", [P, 4, SPLITS, CH], BF16)
        rest = sb("rest", [P, CH])
        st_new = sb("st_new", [QH * HD + 1, NB + 1, HEADS * STRIP])
        st_add = [sb(f"st_add{i}", [QH * HD + 1, HEADS * STRIP]) for i in range(2)]
        y_c = sb("y_c", [P, KC, CH])
        x1c = sb("x1c", [P, NB, DM])
        x2 = sb("x2", [P, NB, DM])
        z3 = sb("z3", [P, NB, DM])
        z3T = sb("z3T", [P, KC, CH])
        w_in = z3[:, 0:KC, :]
        LNS = ("ln1", "ln2", "ln3")
        bnst = {k: sb(f"bnst_{k}", [P, NB, 6]) for k in LNS}
        mv = {k: sb(f"mv_{k}", [P, NB, 2]) for k in LNS}
        var = {k: sb(f"var_{k}", [P, NB]) for k in LNS}
        sd = {k: sb(f"sd_{k}", [P, NB]) for k in LNS}
        rstd = {k: sb(f"rstd_{k}", [P, NB]) for k in LNS}
        shift = {k: sb(f"shift_{k}", [P, NB]) for k in LNS}

        qk_max = sb("qk_max", [P, NCH, 2 * KC])
        qk_top = sb("qk_top", [P, 2 * KC])
        qk_prod = sb("qk_prod", [P, KC])
        head_bound = sb("head_bound", [1, HEADS])
        bound = sb("bound", [1, 1])
        no_low = sb("no_low", [1, 1], mybir.dt.int32)

        score = [ps(f"score{i}", [P, 2, CH]) for i in range(S_BUFS)]
        y_ps = [ps(f"y_ps{i}", [P, CH]) for i in range(2)]
        bank = [ps(f"bank{i}", [P, CH]) for i in range(2)]

        w_loaded = sem("w_loaded")
        const_ready = sem("const_ready")
        setup_pe = sem("setup_pe")
        setup_act = sem("setup_act")
        st_zero = sem("st_zero")
        job_done = sem("job_done")
        emptied = {"act": sem("emptied_act"), "dve": sem("emptied_dve")}
        x_loaded = sem("x_loaded")
        st_loaded = sem("st_loaded")
        x1_stored = sem("x1_stored")
        v_stored = sem("v_stored")
        qT_stored = sem("qT_stored")
        parts_stored = sem("parts_stored")
        st_stored = sem("st_stored")
        c_loaded = sem("c_loaded")
        out_stored = sem("out_stored")
        xb_ready = sem("xb_ready")
        x2b_ready = sem("x2b_ready")
        stats_done = {k: sem(f"stats_{k}") for k in LNS}
        aggr_done = {k: sem(f"aggr_{k}") for k in LNS}
        var_done = {k: sem(f"var_done_{k}") for k in LNS}
        sd_done = {k: sem(f"sd_done_{k}") for k in LNS}
        rstd_done = {k: sem(f"rstd_done_{k}") for k in LNS}
        norm_ready = {k: sem(f"norm_ready_{k}") for k in LNS}
        z_ready = {k: sem(f"z_ready_{k}") for k in LNS}
        split_step = sem("split_step")
        st_added = sem("st_added")
        kv_loaded = [sem(f"kv_loaded{c}") for c in range(CPB)]
        qk_done = sem("qk_done")
        relu_done = sem("relu_done")
        masked = sem("masked")
        poly_done = sem("poly_done")
        pv_done = sem("pv_done")
        y_copied = sem("y_copied")
        y_stored = [sem(f"y_stored{i}") for i in range(2)]

        bounded = sem("bounded")
        bound_step = sem("bound_step")
        bound_ready = sem("bound_ready")
        bound_transposed = sem("bound_transposed")
        low_loaded = sem("low_loaded")
        low_scored = sem("low_scored")
        low_line = sem("low_line")
        low_ready = sem("low_ready")
        low_masked = sem("low_masked")
        low_summed = sem("low_summed")
        low_y_loaded = sem("low_y_loaded")
        low_added = sem("low_added")
        low_stored = sem("low_stored")

        CONSTS = 11
        waits_met = {e.engine: sem(f"waits_met_{i}") for i, e in enumerate((nc.gpsimd, nc.sync, nc.vector))}
        KV_LOADS = SPLITS + len(PAIRS) + 3

        PART_STORES = P // HD

        def phases(eng, body, first=lambda: None, drain=lambda: None, prefetching=False):
            none, all_ = ("done", 0), ("done", NCH)
            body(None, 0, None, None, Counts(A=0, B=none, C=none))
            with eng.Fori(0, AHEAD) as b:
                body(None, b + 1, b, None, Counts(A=b + 1, B=b, C=none))
            first()
            body(0, AHEAD + 1, AHEAD, None, Counts(A=AHEAD + 1, B=AHEAD, C=none), carry=False)
            with eng.Fori(1, BEHIND) as n:
                body(n, n + AHEAD + 1, n + AHEAD, None, Counts(A=n + AHEAD + 1, B=n + AHEAD, C=none))
            with eng.Fori(BEHIND, NCH - AHEAD - 1) as n:
                body(n, n + AHEAD + 1, n + AHEAD, n - BEHIND, Counts(A=n + AHEAD + 1, B=n + AHEAD, C=n - BEHIND))
            n = NCH - AHEAD - 1
            body(n, None, NCH - 1, n - BEHIND, Counts(A=all_, B=NCH - 1, C=n - BEHIND))
            with eng.Fori(NCH - AHEAD, ITERS - prefetching) as n:
                body(n, None, None, n - BEHIND, Counts(A=all_, B=all_, C=n - BEHIND))
            if prefetching:
                n = ITERS - 1
                body(n, None, None, n - BEHIND, Counts(A=all_, B=all_, C=n - BEHIND), prefetch=False)
            drain()
            with eng.Fori(ITERS, ITERS + BEHIND) as n:
                body(None, None, None, n - BEHIND, Counts(A=all_, B=all_, C=n - BEHIND))

        def lows(eng, correct, body):
            eng.wait_ge(bound_ready, 4)
            fine = eng.value_load(no_low[0:1, 0:1], min_val=0, max_val=1)
            with eng.If(fine < 1):
                with eng.Fori(0, ITERS) as n:
                    correct(n)
                with eng.Fori(NCH, 2 * NCH) as c:
                    body(None, None, None, c, Counts(A=("done", NCH), B=("done", NCH), C=c), again=True)
                if eng == nc.sync:
                    eng.wait_ge(out_stored, 16 * 2 * NCH)

        def wait_alone(eng, sem, value):
            eng.wait_ge(sem, value)
            eng.sem_inc(waits_met[eng.engine], 1)

        def wait_emptied(eng, counts, kind, i):
            who, value = counts.emptied(kind, i)
            wait_alone(eng, emptied[who], value) if eng in (nc.gpsimd, nc.sync) else eng.wait_ge(emptied[who], value)

        block = ctx.enter_context(nc.Block())

        @block.sync
        def _(sp):
            sp.dma_start(w_in[:], ffn_w.rearrange("(k p) d -> p k d", p=P)).then_inc(w_loaded, 16)
            sp.dma_start(vr_in[:], ffn_v.rearrange("(k p) r -> p k r", p=P)).then_inc(w_loaded, 16)
            sp.dma_start(c_in[:], ffn_c.rearrange("(k p) r -> p k r", p=P)).then_inc(w_loaded, 16)
            sp.dma_start(w_qkv[:], w_attn.rearrange("(k p) n -> p k n", p=P)).then_inc(w_loaded, 16)
            sp.dma_start(w_out[:], w_proj.rearrange("(k p) n -> p k n", p=P)).then_inc(w_loaded, 16)
            sp.dma_start(bias[:], ffn_b.rearrange("(a n) -> a n", a=1).broadcast_to([P, DM])).then_inc(w_loaded, 16)
            sp.wait_ge(const_ready, 5)
            for b in range(BATCH):
                sp.dma_start(st_d[b, 0], st_new[:, 0, :]).then_inc(st_zero, 16)
            sp.wait_ge(st_zero, 16 * BATCH)

            def load_kv(n, c, where=None):
                b, g = n // QUADS, n % QUADS
                a = b * CPB + c
                cols = slice(CH * c, CH * c + CH)
                where = kv_loaded[c] if where is None else where

                row = 0
                for q_part in range(SPLITS):
                    reps = sum(q == q_part for q, _ in PAIRS)
                    dst = slice(row, row + reps * HD)
                    src = part_d[bass.ds(a, 1), bass.ds((g % 2) * QH, QH), :, bass.ds(g // 2, 1)]
                    sp.dma_start(ks[dst, :, cols], src[:, :, 1, :, 0:reps].rearrange("o h g s d t -> (o g s d) h t")).then_inc(where, 16)
                    for r in range(reps):
                        sp.dma_start(qs[row + r * HD:row + r * HD + HD, :, cols],
                                     src[:, :, 0, :, q_part].rearrange("o h g d t -> (o g d) h t")).then_inc(where, 16)
                    row += reps * HD
                sp.dma_start(vt[:, NB * c:NB * c + NB, :],
                             v_d[bass.ds(a * CH, CH), bass.ds(g * QH * STRIP, QH * STRIP)]
                             .rearrange("(i p) n -> p i n", p=P)).then_inc(where, 16)
                sp.dma_start(qT[0:QH * HD, cols],
                             qT_d[bass.ds(a, 1), bass.ds(g * QH * HD, QH * HD), :]
                             .rearrange("o r t -> (o r) t")).then_inc(where, 16)
                sp.dma_start(st[:, NB * c:NB * c + NB, :],
                             st_d[bass.ds(b, 1), NB * c:NB * c + NB, :, bass.ds(g * QH * STRIP, QH * STRIP)]
                             .rearrange("o m r n -> (o r) m n")).then_inc(where, 16)

            def body(n, a, b, cc, counts, prefetch=True, carry=True, again=False):
                if cc is not None:
                    tok_c = (cc - NCH) * CH if again else cc * CH
                for t in range(NHALF + 1):
                    if a is not None and t == 0:
                        wait_alone(sp, emptied["dve"], counts.base("dve"))
                        sp.dma_start(x_sb[:], x_d[bass.ds(a * CH, CH), :].rearrange("(i p) d -> p i d", p=P)).then_inc(x_loaded, 16)
                    if cc is not None and t == 8:
                        for i in range(2):
                            wait_alone(sp, y_stored[i], (cc + BEHIND if n is not None else ITERS) * (16 * QH * CPB // 2))
                        sp.dma_start(y_c[:], y_d[:, bass.ds(tok_c, CH)].rearrange("(k p) t -> p k t", p=P)).then_inc(c_loaded, 16)
                        sp.dma_start(x1c[:], x1_d[bass.ds(tok_c, CH), :].rearrange("(i p) d -> p i d", p=P)).then_inc(c_loaded, 16)
                    if a is not None and t == 38:
                        wait_emptied(sp, counts, "ffn", 1)
                        sp.dma_start(x1_d[bass.ds(a * CH, CH), :].rearrange("(i p) d -> p i d", p=P), x1[:]).then_inc(x1_stored, 16)
                    if b is not None and t == 20:
                        wait_alone(sp, st_stored, b * 16)
                        sp.dma_start(st_new[:, 0, :], st_d[bass.ds(b // CPB, 1), bass.ds((b % CPB) * NB, 1), :, :]
                                     .rearrange("o m r n -> (o m r) n")).then_inc(st_loaded, 16)
                    if b is not None and t == 50:
                        wait_emptied(sp, counts, "v", 1)
                        sp.dma_start(v_d[bass.ds(b * CH, CH), :].rearrange("(i p) n -> p i n", p=P),
                                     v_sb[:].rearrange("p i h s -> p i (h s)")).then_inc(v_stored, 16)
                    if b is not None and t == 42:
                        wait_emptied(sp, counts, "T", 1)
                        sp.dma_start(qT_d[bass.ds(b, 1), :, :].rearrange("o (g p) t -> (o p) g t", p=P),
                                     qkT[:, 0:2, :]).then_inc(qT_stored, 16)
                    if cc is not None and t == 66:
                        wait_emptied(sp, counts, "out", 1)
                        sp.dma_start(out_d[bass.ds(tok_c, CH), :].rearrange("(i p) d -> p i d", p=P), x2[:]).then_inc(out_stored, 16)
                    if b is not None and t == 58:
                        wait_alone(sp, split_step, (b + 1) * 12)
                        for h in range(P // HD):
                            sp.dma_start(part_d[bass.ds(b, 1), h].rearrange("o w g s d t -> (o d) (w g s) t"),
                                         parts[HD * h:HD * h + HD].rearrange("p g s t -> p (g s) t")).then_inc(parts_stored, 16)
                    if b is not None and t == NHALF:
                        wait_alone(sp, st_added, (b + 1) * NB)
                        sp.dma_start(st_d[bass.ds(b // CPB, 1), bass.ds((b % CPB) * NB + 1, NB), :, :]
                                     .rearrange("o m r n -> (o r) m n"), st_new[:, 1:NB + 1, :]).then_inc(st_stored, 16)
                    if n is not None:
                        for ci in range(CPB):
                            if t == COPY_AT[ci]:
                                store_y(n, ci)
                                if ci == 0:
                                    all_stored(b if b is not None else NCH)
                                if prefetch:
                                    load_kv(n + 1, CPB - 1 - ci)
                            if t == COPY_AT[ci] - NHALF and carry:
                                store_y(n - 1, ci)
                                load_kv(n, CPB - 1 - ci)

            def store_y(n, ci):
                wait_alone(sp, y_copied, n * CPB + (ci + 1))
                for h in range(QH):
                    sp.dma_start(y_d[bass.ds((n % QUADS) * QH * HD + h * HD, HD),
                                     bass.ds((n // QUADS) * SEQ + (CPB - 1 - ci) * CH, CH)],
                                 y_sb[ci % 2][STRIP * h:STRIP * h + HD, :]).then_inc(y_stored[ci % 2], 16)

            def all_stored(chunks):
                wait_alone(sp, v_stored, chunks * 16)
                wait_alone(sp, qT_stored, chunks * 16)
                wait_alone(sp, parts_stored, chunks * (16 * PART_STORES))
                wait_alone(sp, st_stored, chunks * 16)

            def first():
                all_stored(AHEAD)
                for ci in range(CPB):
                    load_kv(0, CPB - 1 - ci)

            phases(sp, body, first, lambda: store_y(ITERS - 1, CPB - 1), prefetching=True)
            sp.wait_ge(out_stored, 16 * NCH)
            sp.wait_ge(x1_stored, 16 * NCH)
            for i in range(2):
                sp.wait_ge(y_stored[i], ITERS * (16 * QH * CPB // 2))

            def correct(n):
                if True:
                    for c in range(CPB):
                        load_kv(n, c, low_loaded)
                for ci in range(CPB):
                    strips = [(y_d[bass.ds((n % QUADS) * QH * HD + h * HD, HD), bass.ds((n // QUADS) * SEQ + (CPB - 1 - ci) * CH, CH)],
                               slice(STRIP * h, STRIP * h + HD)) for h in range(QH)]
                    for dram, rows in strips:
                        sp.dma_start(y_sb[0][rows, :], dram).then_inc(low_y_loaded, 16)
                    wait_alone(sp, low_added, n * CPB + (ci + 1))
                    for dram, rows in strips:
                        sp.dma_start(dram, y_sb[1][rows, :]).then_inc(low_stored, 16)
                    wait_alone(sp, low_stored, (n * CPB + (ci + 1)) * (16 * QH))

            lows(sp, correct, body)

        @block.gpsimd
        def _(pool):
            pool.memset(ident[:], 0.0).then_inc(const_ready, 1)
            pool.memset(smask[:], SLOPE * SCALE).then_inc(const_ready, 1)
            pool.memset(st_new[:], 0.0).then_inc(const_ready, 1)
            pool.memset(v_sb[:], 0.0).then_inc(const_ready, 1)
            pool.memset(ones[:], 1.0).then_inc(const_ready, 1)
            pool.memset(qT[:], 1.0).then_inc(const_ready, 1)
            pool.wait_ge(const_ready, 6)
            pool.affine_select(out=ident[:], in_=ident[:], compare_op=ALU.not_equal, fill=1.0, base=0,
                               pattern=[[-1, P]], channel_multiplier=1).then_inc(const_ready, 1)
            rows = smask[0:QH * HD, :]
            pool.affine_select(out=rows, in_=rows, compare_op=ALU.is_ge, fill=0.0, base=0,
                               pattern=[[0, QUADS], [-HD, QH], [0, STRIP]], channel_multiplier=1).then_inc(const_ready, 1)
            pool.wait_ge(const_ready, 8)
            pool.affine_select(out=rows, in_=rows, compare_op=ALU.is_ge, fill=0.0, base=HD - 1,
                               pattern=[[0, QUADS], [HD, QH], [0, STRIP]], channel_multiplier=-1).then_inc(const_ready, 1)
            pool.memset(smask[QH * HD:QH * HD + 1, :], 1.0).then_inc(const_ready, 1)
            pool.wait_ge(w_loaded, 16 * 6)
            pool.wait_ge(const_ready, 10)
            pool.tensor_scalar(bias_half[:], bias[:], 0.5, 0.0, ALU.mult, ALU.add).then_inc(const_ready, 1)
            pool.wait_ge(const_ready, CONSTS)

            def normalise(k, src, dst, value, i):
                if i == 0:
                    wait_alone(pool, norm_ready[k], value)
                ins = pool.tensor_scalar(dst[:, i, :], src[:, i, :], rstd[k][:, i:i + 1], shift[k][:, i:i + 1],
                                         ALU.mult, ALU.add)
                if i == NB - 1:
                    ins.then_inc(z_ready[k], 1)

            def add_bias(k, x, ready, value, i):
                if i == 0:
                    wait_alone(pool, z_ready[k], value)
                ins = pool.tensor_tensor(x[:, i, :], x[:, i, :], bias_half[:], ALU.add)
                if i == NB - 1:
                    ins.then_inc(ready, 1)

            def body(n, a, b, cc, counts, carry=True, again=False):
                for t in range(NHALF + 1):
                    if n is not None and t // 2 in DIAG:
                        m = DIAG.index(t // 2)
                        off = TILES[t // 2][3]
                        wait_alone(pool, poly_done, n * NHALF + (R_BUFS + t + 1))
                        for buf in (poly[t % (2 * P_BUFS)][:, :, off:off + P], lin[m % 2][:, 2 * (t % 2):2 * (t % 2) + 2, :]):
                            pool.affine_select(out=buf, in_=buf, compare_op=ALU.is_ge, fill=0.0, base=0,
                                               pattern=[[0, 2], [1, P]], channel_multiplier=-1).then_inc(masked, 1)
                    if a is not None:
                        if 0 <= t - LN_AT["ln1"] - NORM < NB:
                            normalise("ln1", x_sb, z, a + 1, t - LN_AT["ln1"] - NORM)
                        if 0 <= t - LN_AT["ln1"] - BIAS < NB:
                            add_bias("ln1", x_sb, xb_ready, a + 1, t - LN_AT["ln1"] - BIAS)
                        if t == LN_AT["ln2"] + NORM:
                            wait_alone(pool, job_done, counts.made("z1T", 1))
                        if 0 <= t - LN_AT["ln2"] - NORM < NB:
                            normalise("ln2", x1, z, a + 1, t - LN_AT["ln2"] - NORM)
                    if cc is not None:
                        if 0 <= t - LN_AT["ln3"] - NORM < NB:
                            normalise("ln3", x2, z3, cc + 1, t - LN_AT["ln3"] - NORM)
                        if 0 <= t - LN_AT["ln3"] - BIAS < NB:
                            add_bias("ln3", x2, x2b_ready, cc + 1, t - LN_AT["ln3"] - BIAS)
                    for _, kind, i, start, who in counts.jobs:
                        step = t - empty_at(kind, start, who) - 1
                        if kind == "T" and 0 <= step < 3:
                            if step == 0:
                                wait_emptied(pool, counts, "T", i)
                                if i == 0:
                                    wait_alone(pool, parts_stored, b * (16 * PART_STORES))
                            wait_alone(pool, split_step, b * 12 + (3 * i + step))
                            if step == 0:
                                pool.tensor_tensor(rest[:], qkT[:, i, :], parts[:, i, 0, :], ALU.subtract).then_inc(split_step, 1)
                            if step == 1:
                                pool.tensor_copy(parts[:, i, 1, :], rest[:]).then_inc(split_step, 1)
                            if step == 2:
                                pool.tensor_tensor(parts[:, i, 2, :], rest[:], parts[:, i, 1, :], ALU.subtract).then_inc(split_step, 1)
                        if kind == "state" and t == min(empty_at(kind, start, who) + 1, NHALF):
                            if i == 0:
                                wait_alone(pool, st_loaded, (b + 1) * 16)
                            else:
                                wait_alone(pool, st_added, b * NB + i)
                            wait_emptied(pool, counts, "state", i)
                            pool.tensor_tensor(st_new[:, i + 1, :], st_new[:, i, :], st_add[i % 2][:], ALU.add).then_inc(st_added, 1)

            phases(pool, body)

            def correct(n):
                for m, t in enumerate(DIAG):
                    for half in range(2):
                        off = TILES[t][3]
                        wait_alone(pool, low_ready, n * NHALF + (2 * t + half + 1))
                        buf = poly[0][:, :, off:off + P]
                        pool.affine_select(out=buf, in_=buf, compare_op=ALU.is_ge, fill=0.0, base=0,
                                           pattern=[[0, 2], [1, P]], channel_multiplier=-1).then_inc(low_masked, 1)

            lows(pool, correct, body)

        @block.scalar
        def _(act):
            act.sem_inc(relu_done, S_BUFS)
            act.wait_ge(setup_pe, 1)
            nc.scalar.activation(vrT[:], score[0][0:32, 0, 0:DM], ACT.Copy).then_inc(setup_act, 1)
            nc.scalar.activation(cT[:], score[0][0:32, 0, DM:2 * DM], ACT.Copy).then_inc(setup_act, 1)
            for k in range(KC):
                act.wait_ge(setup_pe, 2 + k)
                nc.scalar.activation(w_ffn[:, k, :], y_ps[k][:, 0:DM], ACT.Copy, scale=0.5).then_inc(setup_act, 1)
            act.wait_ge(const_ready, CONSTS)

            def root(k, value):
                act.wait_ge(var_done[k], value)
                nc.scalar.activation(sd[k][:], var[k][:], ACT.Sqrt).then_inc(sd_done[k], 1)

            def empty(b, kind, i, src):
                done = emptied["act"]
                if kind in ("z1T", "z2T", "z3T"):
                    dst = {"z1T": zT, "z2T": z2T, "z3T": z3T}[kind]
                    nc.scalar.activation(dst[:, i, :], src[:], ACT.Copy).then_inc(done, 1)
                if kind == "qk":
                    nc.scalar.activation(qk_sb[:, i, :], src[:], ACT.Copy).then_inc(done, 1)
                if kind == "v":
                    if i == 0:
                        act.wait_ge(v_stored, b * 16)
                    nc.scalar.activation(v_sb[:, 2 * i:2 * i + 2, :, 0:HD], src[:].rearrange("p (b h d) -> p b h d", b=2, h=HEADS),
                                         ACT.Copy).then_inc(done, 1)
                if kind == "T":
                    if i == 0:
                        act.wait_ge(qT_stored, b * 16)
                        act.wait_ge(parts_stored, b * (16 * PART_STORES))
                        act.wait_ge(bounded, b * 2 * KC)
                    nc.scalar.activation(qkT[:, i, :], src[:], ACT.Copy)
                    nc.scalar.activation(parts[:, i, 0, :], src[:], ACT.Copy).then_inc(done, 1)

            def body(n, a, b, cc, counts, carry=True, again=False):
                for t in range(NHALF + 1):
                    for k, (_, kind, i, start, who) in enumerate(counts.jobs):
                        if who == "act" and t == empty_at(kind, start, who):
                            act.wait_ge(job_done, counts.made(kind, i))
                            empty(b, kind, i, bank[k % 2])
                    if n is not None and t < NHALF:
                        ci, c, j, off = TILES[t // 2]
                        act.wait_ge(qk_done, n * NHALF + t + 1)
                        if t // 2 in DIAG:
                            act.wait_ge(pv_done, n * NT + t // 2 + 1)
                            nc.scalar.activation(lin[DIAG.index(t // 2) % 2][:, 2 * (t % 2):2 * (t % 2) + 2, :],
                                                 score[t % S_BUFS][:, :, off:off + P], ACT.Copy,
                                                 scale=SLOPE * SCALE, bias=1.0)
                        act.wait_ge(poly_done, n * NHALF + t + 1)
                        nc.scalar.activation(relu[t % R_BUFS][:, :, off:CH], score[t % S_BUFS][:, :, off:CH], ACT.Relu,
                                             scale=SCALE).then_inc(relu_done, 1)
                    for ci in range(CPB):
                        if n is not None and t == COPY_AT[ci]:
                            copy_y(n, ci)
                        if n is not None and t == COPY_AT[ci] - NHALF and carry:
                            copy_y(n - 1, ci)
                    if a is not None and t == LN_AT["ln1"] + ROOT:
                        root("ln1", a + 1)
                    if a is not None and t == LN_AT["ln2"] + ROOT:
                        root("ln2", a + 1)
                    if cc is not None and t == LN_AT["ln3"] + ROOT:
                        root("ln3", cc + 1)

            def copy_y(n, ci):
                act.wait_ge(pv_done, n * NT + (P_BUFS + LAST[ci] + 1))
                act.wait_ge(y_stored[ci % 2], n * (16 * QH * CPB // 2) + (ci // 2) * 16 * QH)
                nc.scalar.activation(y_sb[ci % 2][:], y_ps[ci % 2][:], ACT.Copy).then_inc(y_copied, 1)

            phases(act, body, drain=lambda: copy_y(ITERS - 1, CPB - 1))
            lows(act, lambda n: None, body)

        @block.vector
        def _(dve):
            dve.sem_inc(poly_done, R_BUFS)
            dve.wait_ge(const_ready, CONSTS)

            def stats(k, src, value, i):
                nc.vector.bn_stats(bnst[k][:, i, :], src[:, i, :]).then_inc(stats_done[k], 1)

            def aggregate(k, value):
                wait_alone(dve, stats_done[k], (value + 1) * NB)
                for i in range(NB):
                    nc.vector.bn_aggr(mv[k][:, i, :], bnst[k][:, i, :]).then_inc(aggr_done[k], 1)
                dve.wait_ge(aggr_done[k], (value + 1) * NB)
                nc.vector.tensor_scalar(var[k][:], mv[k][:, :, 1], EPS, None, ALU.add).then_inc(var_done[k], 1)

            def scales(k, value):
                dve.wait_ge(sd_done[k], value + 1)
                nc.vector.reciprocal(rstd[k][:], sd[k][:]).then_inc(rstd_done[k], 1)
                dve.wait_ge(rstd_done[k], value + 1)
                nc.vector.scalar_tensor_tensor(shift[k][:], mv[k][:, :, 0], -1.0, rstd[k][:], ALU.mult, ALU.mult).then_inc(norm_ready[k], 1)

            def empty(a, b, cc, kind, i, src):
                done = emptied["dve"]
                two = src[:].rearrange("p (b d) -> p b d", b=2)
                if kind == "ffn":
                    if i == 0:
                        dve.wait_ge(xb_ready, a + 1)
                        dve.wait_ge(x1_stored, a * 16)
                    nc.vector.tensor_tensor(x1[:, 2 * i:2 * i + 2, :], two, x_sb[:, 2 * i:2 * i + 2, :], ALU.add).then_inc(done, 1)
                if kind == "proj":
                    if i == 0:
                        dve.wait_ge(c_loaded, (cc + 1) * 32)
                        dve.wait_ge(out_stored, cc * 16)
                    nc.vector.scalar_tensor_tensor(x2[:, 2 * i:2 * i + 2, :], two, 1.0 / DIVISOR, x1c[:, 2 * i:2 * i + 2, :],
                                                   ALU.mult, ALU.add).then_inc(done, 1)
                if kind == "out":
                    if i == 0:
                        dve.wait_ge(x2b_ready, cc + 1)
                    nc.vector.tensor_tensor(x2[:, 2 * i:2 * i + 2, :], two, x2[:, 2 * i:2 * i + 2, :], ALU.add).then_inc(done, 1)
                if kind == "state":
                    if i >= 2:
                        dve.wait_ge(st_added, b * NB + i - 1)
                    nc.vector.tensor_tensor(st_add[i % 2][:], src[0:QH * HD + 1, :], smask[:], ALU.mult).then_inc(done, 1)

            def body(n, a, b, cc, counts, carry=True, again=False):
                for t in range(NHALF + 1):
                    for k, (_, kind, i, start, who) in enumerate(counts.jobs):
                        if who == "dve" and t == empty_at(kind, start, who):
                            dve.wait_ge(job_done, counts.made(kind, i))
                            empty(a, b, cc, kind, i, bank[k % 2])
                    if n is not None and t < NHALF:
                        ci, c, j, off = TILES[t // 2]
                        dve.wait_ge(relu_done, n * NHALF + (S_BUFS + t + 1))
                        if t % 2 == 0:
                            dve.wait_ge(pv_done, n * NT + t // 2 + 1)
                        r = relu[t % R_BUFS][:, :, off:CH]
                        nc.vector.scalar_tensor_tensor(poly[t % (2 * P_BUFS)][:, :, off:CH], r, -SLOPE, r,
                                                       ALU.add, ALU.mult).then_inc(poly_done, 1)
                    for _, kind, i, start, who in counts.jobs:
                        if kind == "T" and t == empty_at(kind, start, who) + 1:
                            wait_emptied(dve, counts, "T", i)
                            nc.vector.tensor_reduce(qk_max[:, bass.ds(b, 1), i:i + 1].rearrange("p c g -> p (c g)"), qkT[:, i, :],
                                                    AX.X, ALU.max, apply_absolute_value=True).then_inc(bounded, 1)
                    for k, chunk, x in (("ln1", a, x_sb), ("ln2", a, x1), ("ln3", cc, x2)):
                        if chunk is None:
                            continue
                        step = t - LN_AT[k]
                        if step == 0:
                            if k == "ln1":
                                dve.wait_ge(x_loaded, (a + 1) * 16)
                            else:
                                wait_emptied(dve, counts, "ffn" if k == "ln2" else "proj", 1)
                        if 0 <= step < NB:
                            stats(k, x, chunk, step)
                        if step == AGGR:
                            aggregate(k, chunk)
                        if step == SCALES:
                            scales(k, chunk)

            phases(dve, body)

            dve.wait_ge(bounded, NCH * 2 * KC)
            nc.vector.tensor_reduce(qk_top[:], qk_max[:].rearrange("p c g -> p g c"), AX.X, ALU.max).then_inc(bound_ready, 1)
            dve.wait_ge(bound_ready, 1)
            nc.vector.tensor_tensor(qk_prod[:], qk_top[:, 0:KC], qk_top[:, KC:2 * KC], ALU.mult).then_inc(bound_step, 1)
            dve.wait_ge(bound_transposed, 1)
            nc.vector.tensor_reduce(head_bound[:], bank[0][0:1, 0:DM].rearrange("p (h d) -> p h d", h=HEADS), AX.X, ALU.add).then_inc(bound_ready, 1)
            dve.wait_ge(bound_ready, 2)
            nc.vector.tensor_reduce(bound[:], head_bound[:], AX.X, ALU.max).then_inc(bound_ready, 1)
            dve.wait_ge(bound_ready, 3)
            nc.vector.tensor_scalar(no_low[:], bound[:], BOUND, None, ALU.is_lt).then_inc(bound_ready, 1)

            def correct(n):
                for h in range(NHALF):
                    ci, c, j, off = TILES[h // 2]
                    s = score[0][:, :, off:CH]
                    dve.wait_ge(low_scored, n * NHALF + (h + 1))
                    nc.vector.tensor_scalar(relu[0][:, :, off:CH], s, -SLOPE * SCALE, -1.0, ALU.mult, ALU.add).then_inc(low_line, 1)
                    dve.wait_ge(low_line, n * NHALF + (h + 1))
                    nc.vector.scalar_tensor_tensor(poly[0][:, :, off:CH], s, X_INT / SCALE, relu[0][:, :, off:CH],
                                                   ALU.is_lt, ALU.mult).then_inc(low_ready, 1)
                    if h == 2 * LAST[ci] + 1:
                        dve.wait_ge(low_summed, n * CPB + (ci + 1))
                        dve.wait_ge(low_y_loaded, (n * CPB + (ci + 1)) * (16 * QH))
                        nc.vector.tensor_tensor(y_sb[1][:], y_ps[0][:], y_sb[0][:], ALU.add).then_inc(low_added, 1)

            lows(dve, correct, body)

        @block.tensor
        def _(pe):
            def mm(*args, start=True, stop=True):
                return nc.tensor.matmul(*args, start=start, stop=stop, skip_group_check=True)

            pe.sem_inc(pv_done, P_BUFS)
            pe.wait_ge(const_ready, CONSTS)
            pe.wait_ge(w_loaded, 16 * 6)
            for k in range(KC):
                nc.tensor.transpose(score[0][0:32, 0, P * k:P * k + P], vr_in[:, k, :], ident[:])
                ins = nc.tensor.transpose(score[0][0:32, 0, DM + P * k:DM + P * k + P], c_in[:, k, :], ident[:])
            ins.then_inc(setup_pe, 1)
            pe.wait_ge(setup_act, 2)
            for k in range(KC):
                for o in range(KC):
                    dst = y_ps[k][:, P * o:P * o + P]
                    mm(dst, w_in[:, o, P * k:P * k + P], ident[:], start=True, stop=False)
                    ins = mm(dst, vrT[:, P * k:P * k + P], cT[:, P * o:P * o + P], start=False, stop=True)
                ins.then_inc(setup_pe, 1)
            pe.wait_ge(setup_act, 4)

            def transposes(dst, src, i):
                for blk in range(NB):
                    ins = nc.tensor.transpose(dst[:, P * blk:P * blk + P], src[:, blk, P * i:P * i + P], ident[:])
                return ins

            def job(a, b, cc, counts, k, kind, i, piece):
                dst = bank[k % 2]
                if piece == 0:
                    if k < 2:
                        for who in ("act", "dve"):
                            pe.wait_ge(emptied[who], counts.base(who))
                    else:
                        wait_emptied(pe, counts, counts.jobs[k - 2][1], counts.jobs[k - 2][2])
                first = piece == 0 and i == 0
                half = dst[:, DM * (piece // 2):DM * (piece // 2) + DM]
                kc = piece % 2
                if kind in ("z1T", "z2T", "z3T"):
                    name = {"z1T": "ln1", "z2T": "ln2", "z3T": "ln3"}[kind]
                    if first:
                        pe.wait_ge(z_ready[name], (cc if kind == "z3T" else a) + 1)
                    ins = transposes(dst, z3 if kind == "z3T" else z, i)
                if kind in ("ffn", "out", "proj", "v"):
                    if first and kind == "proj":
                        pe.wait_ge(c_loaded, (cc + 1) * 32)
                    if first and kind in ("ffn", "out"):
                        wait_emptied(pe, counts, {"ffn": "z1T", "out": "z3T"}[kind], 1)
                    src, w = {"ffn": (zT, w_ffn), "out": (z3T, w_ffn), "proj": (y_c, w_out), "v": (z2T, w_qkv[:, :, 2 * DM:])}[kind]
                    blk = 2 * i + piece // 2
                    ins = mm(half, src[:, kc, P * blk:P * blk + P], w[:, kc, :], start=kc == 0, stop=kc == KC - 1)
                if kind == "qk":
                    if first:
                        pe.wait_ge(emptied["act"], counts.base("act"))
                    cols = slice(DM * (piece // 2), DM * (piece // 2) + DM)
                    ins = mm(half, z2T[:, kc, P * i:P * i + P], w_qkv[:, kc, cols], start=kc == 0, stop=kc == KC - 1)
                if kind == "T":
                    if first:
                        wait_emptied(pe, counts, "qk", 3)
                    ins = transposes(dst, qk_sb, i)
                if kind == "state":
                    if first:
                        wait_emptied(pe, counts, "v", 1)
                    v_row = v_sb[:, i].rearrange("p h s -> p (h s)")
                    for g in range(2 * piece, min(2 * piece + 2, QUADS)):
                        k_cols = qk_sb[:, i, DM + QH * HD * g:DM + QH * HD * (g + 1)]
                        ins = mm(dst[0:QH * HD, P * g:P * g + P], k_cols, v_row[:, P * g:P * g + P])
                    if piece == 2:
                        ins = mm(dst[QH * HD:QH * HD + 1, :], ones[:], v_row)
                if piece == PIECES[kind] - 1:
                    ins.then_inc(job_done, 1)

            def score_half(n, h):
                ci, c, j, off = TILES[h // 2]
                if h % 2 == 0 and j // NB not in [x[2] // NB for x in TILES[:h // 2]]:
                    pe.wait_ge(kv_loaded[j // NB], (n + 1) * (16 * KV_LOADS))
                pe.wait_ge(relu_done, n * NHALF + h + 1)
                for u in range(2):
                    head = 2 * (h % 2) + u
                    ins = mm(score[h % S_BUFS][:, u, off:CH], ks[:, head, P * j:P * j + P],
                             qs[:, head, CH * c + off:CH * c + CH])
                ins.then_inc(qk_done, 1)

            def values(n, t):
                ci, c, j, off = TILES[t]
                y = y_ps[ci % 2]
                if t == FIRST[ci]:
                    if ci >= 2 or not (isinstance(n, int) and n == 0):
                        pe.wait_ge(y_copied, n * CPB + (ci - 1))
                    for m in range(NB):
                        mm(y[:, P * m:P * m + P], st[:, NB * c + m, :], qT[:, CH * c + P * m:CH * c + P * m + P],
                           start=m == 0, stop=False)
                if t in DIAG:
                    pe.wait_ge(masked, n * 4 * len(DIAG) + (4 * DIAG.index(t) + 4))
                else:
                    pe.wait_ge(poly_done, n * NHALF + (R_BUFS + 2 * t + 2))
                last = t == LAST[ci]
                for head in range(QH):
                    ins = mm(y[STRIP * head:STRIP * head + HD, off:CH], vt[:, j, STRIP * head:STRIP * head + HD],
                             poly[(2 * t + head // 2) % (2 * P_BUFS)][:, head % 2, off:CH], start=False, stop=last)
                if t in DIAG:
                    for head in range(QH):
                        ins = mm(y[STRIP * head:STRIP * head + HD, off:off + P], vt[:, j, STRIP * head:STRIP * head + HD],
                                 lin[DIAG.index(t) % 2][:, head, :], start=False, stop=False)
                ins.then_inc(pv_done, 1)

            def body(n, a, b, cc, counts, carry=True, again=False):
                for t in range(NHALF):
                    if n is not None:
                        score_half(n, t)
                        if t % 2 == 0 and t // 2 >= LAG:
                            values(n, t // 2 - LAG)
                        elif t % 2 == 0 and carry:
                            values(n - 1, t // 2 - LAG + NT)
                    for k, (_, kind, i, start, _) in enumerate(counts.jobs):
                        if 0 <= t - start < PIECES[kind]:
                            job(a, b, cc, counts, k, kind, i, t - start)

            def drain():
                for t in range(NT - LAG, NT):
                    values(ITERS - 1, t)

            phases(pe, body, drain=drain)

            pe.wait_ge(bound_step, 1)
            for who, jobs in (("act", sum(x[4] == "act" for x in JOBS)), ("dve", sum(x[4] == "dve" for x in JOBS))):
                pe.wait_ge(emptied[who], NCH * jobs)
            for g in range(KC):
                ins = nc.tensor.transpose(bank[0][0:1, P * g:P * g + P], qk_prod[:, g:g + 1], ident[:])
            ins.then_inc(bound_transposed, 1)

            def correct(n):
                pe.wait_ge(low_loaded, (n + 1) * (16 * KV_LOADS * CPB))
                for h in range(NHALF):
                    ci, c, j, off = TILES[h // 2]
                    y = y_ps[0]
                    if h == 2 * FIRST[ci]:
                        if ci == 0:
                            pe.wait_ge(low_added, n * CPB)
                        else:
                            pe.wait_ge(low_added, n * CPB + ci)
                        mm(y[:], st[:, 0, :], qT[:, 0:CH], start=True, stop=False)
                    for u in range(2):
                        head = 2 * (h % 2) + u
                        ins = mm(score[0][:, u, off:CH], ks[:, head, P * j:P * j + P], qs[:, head, CH * c + off:CH * c + CH])
                    ins.then_inc(low_scored, 1)
                    pe.wait_ge(low_ready, n * NHALF + (h + 1))
                    if h // 2 in DIAG:
                        pe.wait_ge(low_masked, n * (2 * len(DIAG)) + (2 * DIAG.index(h // 2) + h % 2 + 1))
                    for u in range(2):
                        head = 2 * (h % 2) + u
                        ins = mm(y[STRIP * head:STRIP * head + HD, off:CH], vt[:, j, STRIP * head:STRIP * head + HD],
                                 poly[0][:, u, off:CH], start=False, stop=h == 2 * LAST[ci] + 1)
                    if h == 2 * LAST[ci] + 1:
                        ins.then_inc(low_summed, 1)

            lows(pe, correct, body)


_INS = ['L0_attn_x', 'L0_attn_W_attn', 'L0_attn_W_proj', 'L0_ffn_W', 'L0_ffn_b', 'L0_ffn_V_r', 'L0_ffn_C']
_OUTS = [((BATCH, SEQ, DM), 'float32')]


def kernel(**inputs):
    import numpy as _np
    import concourse.bacc as _bacc
    from concourse import mybir as _mybir
    from concourse.bass_utils import run_bass_kernel_spmd as _run

    nc = _bacc.Bacc("TRN2", target_bir_lowering=False, num_devices=1)
    arrays, args = {}, []
    for name in _INS:
        a = _np.ascontiguousarray(inputs[name])
        arrays[f"in_{name}_dram"] = a
        args.append(nc.dram_tensor(f"in_{name}_dram", a.shape, _mybir.dt.from_np(a.dtype), kind="ExternalInput").ap())
    for i, (shape, dtype) in enumerate(_OUTS):
        dt = _mybir.dt.from_np(_np.dtype(dtype))
        args.append(nc.dram_tensor(f"out_{i}_dram", shape, dt, kind="ExternalOutput").ap())
    build(nc, *args)
    r = _run(nc, [arrays], core_ids=[0])
    return r.results[0]["out_0_dram"]
```

```python
from contextlib import ExitStack

import concourse.bass as bass
from concourse import mybir

F32 = mybir.dt.float32
BF16 = mybir.dt.bfloat16
ALU = mybir.AluOpType
ACT = mybir.ActivationFunctionType
AX = mybir.AxisListType

P = 128
BATCH, SEQ, DM = 4, 2048, 256
HEADS, HD = 16, 16
KC = DM // P
CH = 512
NB = CH // P
NCH = BATCH * SEQ // CH
CPB = SEQ // CH
QH = 4
QUADS = HEADS // QH
ITERS = BATCH * QUADS
RANK = 32
STRIP = 32
SPLITS = 3
PAIRS = [(0, 0), (0, 1), (0, 2), (1, 0), (1, 1), (2, 0)]
KROWS = len(PAIRS) * HD
EPS = 1e-5
SCALE = HD ** -0.5
X_INT = -100.0
SLOPE = 1.0 / X_INT
BOUND = 0.99 * -X_INT / SCALE
DIVISOR = 1000.0
AHEAD, BEHIND = CPB, CPB

S_BUFS, R_BUFS, P_BUFS, L_BUFS = 2, 4, 3, 4
LAG = 2

TILES = []
for ci in range(CPB):
    c = CPB - 1 - ci
    for m in range(NB):
        TILES.append((ci, c, NB * c + m, P * m))
        TILES += [(ci, c, NB * c - 1 - c * m - i, 0) for i in range(c)]
NT = len(TILES)
NHALF = 2 * NT
DIAG = [t for t, (ci, c, j, off) in enumerate(TILES) if j >= NB * c]
FIRST = [next(t for t, x in enumerate(TILES) if x[0] == ci) for ci in range(CPB)]
LAST = [max(t for t, x in enumerate(TILES) if x[0] == ci) for ci in range(CPB)]

POLY_BUF = [t % P_BUFS for t in range(NT)]
if NT % P_BUFS == 1:
    POLY_BUF[-1] = 1
BASE = 16
PV_BASE = 6


def since(users, t):
    return min([(t - x - 1) % NT + 1 for x in users] + [PV_BASE])


def pv_used(n, users, t):
    return n * NT + (PV_BASE + t + 1 - since(users, t))


def same_poly(t):
    return [x for x in range(NT) if POLY_BUF[x] == POLY_BUF[t]]


def same_lin(t):
    return DIAG[DIAG.index(t) % L_BUFS::L_BUFS]


def lin_made(n, h):
    return n * 2 * len(DIAG) + (S_BUFS + 2 * DIAG.index(h // 2) + h % 2 + 1)


JOBS = [
    ("B", "qk", 0, 0, "act"), ("B", "qk", 1, 4, "act"), ("B", "qk", 2, 8, "act"), ("B", "qk", 3, 12, "act"),
    ("B", "v", 0, 16, "act"), ("B", "v", 1, 20, "act"),
    ("C", "proj", 0, 24, "dve"), ("C", "proj", 1, 28, "dve"),
    ("B", "T", 0, 32, "act"), ("B", "state", 0, 34, "dve"),
    ("B", "T", 1, 37, "act"), ("B", "state", 1, 39, "dve"),
    ("B", "T", 2, 42, "act"), ("A", "z1T", 0, 44, "act"),
    ("B", "state", 2, 45, "dve"), ("A", "z1T", 1, 48, "act"),
    ("B", "T", 3, 50, "act"), ("B", "state", 3, 51, "dve"),
    ("A", "ffn", 0, 54, "dve"), ("A", "ffn", 1, 58, "dve"),
    ("D", "z3T", 0, 62, "act"), ("D", "z3T", 1, 64, "act"),
    ("D", "out", 0, 67, "dve"), ("D", "out", 1, 71, "dve"),
    ("A", "z2T", 0, 76, "act"), ("A", "z2T", 1, 78, "act"),
]
JOBS_EARLY = [
    ("B", "qk", 0, 0, "act"), ("B", "qk", 1, 4, "act"), ("B", "qk", 2, 8, "act"), ("B", "qk", 3, 12, "act"),
    ("A", "z1T", 0, 16, "act"), ("A", "z1T", 1, 18, "act"),
    ("A", "ffn", 0, 20, "dve"), ("A", "ffn", 1, 24, "dve"),
    ("B", "v", 0, 28, "act"), ("B", "v", 1, 32, "act"),
    ("B", "T", 0, 36, "act"), ("B", "state", 0, 38, "dve"),
    ("B", "T", 1, 41, "act"), ("B", "state", 1, 43, "dve"),
    ("B", "T", 2, 46, "act"), ("B", "state", 2, 48, "dve"),
    ("B", "T", 3, 51, "act"), ("B", "state", 3, 53, "dve"),
    ("A", "z2T", 0, 76, "act"), ("A", "z2T", 1, 78, "act"),
]
SPLIT = (1, 6, 6)
PIECES = {"z1T": 1, "z2T": 1, "z3T": 1, "T": 1, "state": 2, "ffn": 4, "out": 4, "proj": 4, "qk": 4, "v": 4}
LN_AT = {"ln1": 8, "ln3": 32, "ln2": 61}
LN_EARLY = {"ln1": 0, "ln3": 32, "ln2": 27}
AGGR, ROOT, SCALES, NORM, BIAS = NB, NB + 4, NB + 3, NB + 4, 2 * NB + 4
COPY_AT = [2 * (LAST[ci] + LAG) + 1 for ci in range(CPB)]


def empty_at(kind, start, who):
    return start + PIECES[kind] + (1 if who == "act" else -1)


class Counts:

    def __init__(self, jobs=JOBS, **stages):
        self.jobs = [x for x in jobs if not isinstance(stages[x[0]], tuple)]
        self.before = {k: v[1] if isinstance(v, tuple) else v for k, v in stages.items()}

    def base(self, by=None):
        per = {stage: sum(x[0] == stage and by in (None, x[4]) for x in JOBS) for stage in "ABCD"}
        return sum(self.before[stage] * per[stage] for stage in "ABCD")

    def local(self, kind, i, by=None):
        n = 0
        for _, k, x, _, who in self.jobs:
            n += by in (None, who)
            if (k, x) == (kind, i):
                return n
        raise KeyError(kind)

    def made(self, kind, i):
        return self.base() + self.local(kind, i)

    def emptied(self, kind, i):
        who = next(x[4] for x in self.jobs if (x[1], x[2]) == (kind, i))
        return who, self.base(who) + self.local(kind, i, who)


def build(nc, x_in, w_attn, w_proj, ffn_w, ffn_b, ffn_v, ffn_c, out):
    ctx = ExitStack()
    with ctx:
        def sb(name, shape, dt=F32):
            return ctx.enter_context(nc.sbuf_tensor(name, shape, dt))

        def ps(name, shape, dt=F32):
            return ctx.enter_context(nc.psum_tensor(name, shape, dt))

        def sem(name):
            return ctx.enter_context(nc.semaphore(name))

        x_d = x_in.rearrange("b t d -> (b t) d")
        out_d = out.rearrange("b t d -> (b t) d")
        x1_d = nc.dram_tensor("x1_scratch", [NCH * CH, DM], F32, kind="Internal").ap()
        part_d = nc.dram_tensor("part_scratch", [NCH, P // HD, 2, KC, SPLITS, HD, CH], BF16, kind="Internal").ap()
        qT_d = nc.dram_tensor("qT_scratch", [NCH, DM, CH], F32, kind="Internal").ap()
        v_d = nc.dram_tensor("v_scratch", [NCH * CH, HEADS * STRIP], F32, kind="Internal").ap()
        st_d = nc.dram_tensor("state_scratch", [BATCH, CPB * NB + 1, QH * HD + 1, HEADS * STRIP], F32, kind="Internal").ap()
        y_d = nc.dram_tensor("y_scratch", [DM, NCH * CH], F32, kind="Internal").ap()

        ident = sb("ident", [P, P])
        ones = sb("ones", [P, 1])
        w_ffn = sb("w_ffn", [P, KC, DM])
        w_qkv = sb("w_qkv", [P, KC, 3 * DM])
        w_out = sb("w_out", [P, KC, DM])
        bias_half = sb("bias_half", [P, DM])
        smask = sb("smask", [QH * HD + 1, DM])
        qs = sb("qs", [KROWS, QH, SEQ], BF16)
        ks = sb("ks", [KROWS, QH, SEQ], BF16)
        vt = sb("vt", [P, SEQ // P, QH * STRIP])
        qT = sb("qT", [QH * HD + 1, SEQ])
        st = sb("st", [QH * HD + 1, SEQ // P, QH * STRIP])
        relu = [sb(f"relu{i}", [P, 2, CH]) for i in range(R_BUFS)]
        poly = [sb(f"poly{i}", [P, 2, CH]) for i in range(2 * P_BUFS)]
        lin = [sb(f"lin{i}", [P, QH, P]) for i in range(L_BUFS)]
        vr_in, c_in = [relu[0][:, i, 0:KC * RANK].rearrange("p (k r) -> p k r", k=KC) for i in range(2)]
        vrT, cT = [relu[1][0:RANK, i, 0:DM] for i in range(2)]
        y_sb = [sb(f"y_sb{i}", [P, CH]) for i in range(2)]
        x_sb = sb("x_sb", [P, NB, DM])
        x1 = sb("x1", [P, NB, DM])
        z = sb("z", [P, NB, DM])
        zT = sb("zT", [P, KC, CH])
        z2T = sb("z2T", [P, KC, CH])
        qk_sb = sb("qk_sb", [P, NB, 2 * DM])
        v_sb = sb("v_sb", [P, NB, HEADS, STRIP])
        qkT = sb("qkT", [P, 4, CH])
        parts = sb("parts", [P, 4, SPLITS, CH], BF16)
        rest = sb("rest", [P, CH])
        st_new = sb("st_new", [QH * HD + 1, NB + 1, HEADS * STRIP])
        st_add = [sb(f"st_add{i}", [QH * HD + 1, DM]) for i in range(2)]
        y_c = sb("y_c", [P, KC, CH])
        x1c = sb("x1c", [P, NB, DM])
        x2 = sb("x2", [P, NB, DM])
        z3 = sb("z3", [P, NB, DM])
        z3T = zT
        w_in = z3[:, 0:KC, :]
        LNS = ("ln1", "ln2", "ln3")
        bnst = {k: sb(f"bnst_{k}", [P, NB, 6]) for k in LNS}
        mv = {k: sb(f"mv_{k}", [P, NB, 2]) for k in LNS}
        var = {k: sb(f"var_{k}", [P, NB]) for k in LNS}
        sd = {k: sb(f"sd_{k}", [P, NB]) for k in LNS}
        rstd = {k: sb(f"rstd_{k}", [P, NB]) for k in LNS}
        shift = {k: sb(f"shift_{k}", [P, NB]) for k in LNS}

        qk_max = sb("qk_max", [P, NCH, 2 * KC])
        qk_top = sb("qk_top", [P, 2 * KC])
        qk_prod = sb("qk_prod", [P, KC])
        head_bound = sb("head_bound", [1, HEADS])
        bound = sb("bound", [1, 1])
        no_low = sb("no_low", [1, 1], mybir.dt.int32)

        def c_bufs(c, last):
            if last and c % 2:
                return z2T, x_sb, x1, z, qkT[:, 0:KC], "ln1"
            return y_c, x1c, x2, z3, z3T, "ln3"

        def c_load(c, last, again=False):
            if last and c % 2:
                return odd_loaded, (c - (NCH - BEHIND) + 1) // 2 * 32
            if last:
                return c_loaded, (NCH - BEHIND + (c - (NCH - BEHIND)) // 2 + 1) * 32
            return c_loaded, (c + (1 - BEHIND // 2 if again else 1)) * 32

        score = [ps(f"score{i}", [P, 2, CH]) for i in range(S_BUFS)]
        y_ps = [ps(f"y_ps{i}", [P, CH]) for i in range(2)]
        bank = [ps(f"bank{i}", [P, CH]) for i in range(2)]

        w_loaded = sem("w_loaded")
        const_ready = sem("const_ready")
        setup_pe = sem("setup_pe")
        setup_act = sem("setup_act")
        st_zero = sem("st_zero")
        job_done = sem("job_done")
        emptied = {"act": sem("emptied_act"), "dve": sem("emptied_dve")}
        x_loaded = sem("x_loaded")
        st_loaded = sem("st_loaded")
        x1_stored = sem("x1_stored")
        v_stored = sem("v_stored")
        qT_stored = sem("qT_stored")
        parts_stored = sem("parts_stored")
        st_stored = sem("st_stored")
        c_loaded = sem("c_loaded")
        odd_loaded = sem("odd_loaded")
        out_stored = sem("out_stored")
        xb_ready = sem("xb_ready")
        x2b_ready = sem("x2b_ready")
        stats_done = {k: sem(f"stats_{k}") for k in LNS}
        aggr_done = {k: sem(f"aggr_{k}") for k in LNS}
        var_done = {k: sem(f"var_done_{k}") for k in LNS}
        sd_done = {k: sem(f"sd_done_{k}") for k in LNS}
        rstd_done = {k: sem(f"rstd_done_{k}") for k in LNS}
        norm_ready = {k: sem(f"norm_ready_{k}") for k in LNS}
        z_ready = {k: sem(f"z_ready_{k}") for k in LNS}
        split_step = sem("split_step")
        st_added = sem("st_added")
        kv_loaded = [sem(f"kv_loaded{c}") for c in range(CPB)]
        qk_done = sem("qk_done")
        relu_done = sem("relu_done")
        lin_done = sem("lin_done")
        masked = sem("masked")
        poly_done = sem("poly_done")
        pv_done = sem("pv_done")
        y_copied = sem("y_copied")
        y_stored = [sem(f"y_stored{i}") for i in range(2)]

        bounded = sem("bounded")
        bound_step = sem("bound_step")
        bound_ready = sem("bound_ready")
        bound_transposed = sem("bound_transposed")
        low_loaded = sem("low_loaded")
        low_scored = sem("low_scored")
        low_line = sem("low_line")
        low_ready = sem("low_ready")
        low_masked = sem("low_masked")
        low_summed = sem("low_summed")
        low_y_loaded = sem("low_y_loaded")
        low_added = sem("low_added")
        low_stored = sem("low_stored")

        CONSTS = 11
        waits_met = {e.engine: sem(f"waits_met_{i}") for i, e in enumerate((nc.gpsimd, nc.sync, nc.vector))}
        KV_LOADS = SPLITS + len(PAIRS) + 3

        PART_STORES = P // HD

        def phases(eng, body, early=lambda: None, first=lambda: None, drain=lambda: None,
                   prefetching=False):
            none, all_ = ("done", 0), ("done", NCH)
            body(None, 0, None, None, None, Counts(JOBS_EARLY, A=0, B=none, C=none, D=none))
            with eng.Fori(0, AHEAD - prefetching) as b:
                body(None, b + 1, b, None, None, Counts(JOBS_EARLY, A=b + 1, B=b, C=none, D=none))
            if prefetching:
                early()
                body(None, AHEAD, AHEAD - 1, None, None, Counts(JOBS_EARLY, A=AHEAD, B=AHEAD - 1, C=none, D=none))
            first()
            body(0, AHEAD + 1, AHEAD, None, None, Counts(A=AHEAD + 1, B=AHEAD, C=none, D=none), carry=False)
            with eng.Fori(1, BEHIND) as n:
                a, b = n + AHEAD + 1, n + AHEAD
                body(n, a, b, None, None, Counts(A=a, B=b, C=none, D=none))
            with eng.Fori(BEHIND, NCH - AHEAD - 1 - prefetching) as n:
                a, b, c = n + AHEAD + 1, n + AHEAD, n - BEHIND
                body(n, a, b, c, c, Counts(A=a, B=b, C=c, D=c))
            if prefetching:
                n = NCH - AHEAD - 2
                c = n - BEHIND
                body(n, NCH - 1, NCH - 2, c, c, Counts(A=NCH - 1, B=NCH - 2, C=c, D=c), next_x=False)
            n = NCH - AHEAD - 1
            c = n - BEHIND
            body(n, None, NCH - 1, c, c, Counts(A=all_, B=NCH - 1, C=c, D=c))
            with eng.Fori(NCH - AHEAD, ITERS - prefetching) as n:
                c = n - BEHIND
                body(n, None, None, c, c, Counts(A=all_, B=all_, C=c, D=c))
            if prefetching:
                n = ITERS - 1
                c = n - BEHIND
                body(n, None, None, c, c, Counts(A=all_, B=all_, C=c, D=c), prefetch=False)
            drain()
            for c in range(NCH - BEHIND, NCH + 1):
                d = c - 1
                body(None, None, None, c if c < NCH else None, d if c > NCH - BEHIND else None,
                     Counts(A=all_, B=all_, C=c if c < NCH else all_, D=d if c > NCH - BEHIND else ("done", NCH - BEHIND)),
                     last=True)

        def lows(eng, correct, body):
            eng.wait_ge(bound_ready, 4)
            fine = eng.value_load(no_low[0:1, 0:1], min_val=0, max_val=1)
            with eng.If(fine < 1):
                with eng.Fori(0, ITERS) as n:
                    correct(n)
                with eng.Fori(NCH, 2 * NCH) as c:
                    body(None, None, None, c, c, Counts(A=("done", NCH), B=("done", NCH), C=c, D=c), again=True)
                if eng == nc.sync:
                    eng.wait_ge(out_stored, 16 * 2 * NCH + BASE)

        def wait_alone(eng, sem, value):
            eng.wait_ge(sem, value)
            eng.sem_inc(waits_met[eng.engine], 1)

        def wait_emptied(eng, counts, kind, i):
            who, value = counts.emptied(kind, i)
            wait_alone(eng, emptied[who], value) if eng in (nc.gpsimd, nc.sync) else eng.wait_ge(emptied[who], value)

        def split(eng, b, counts, i, step):
            if step == 0:
                wait_emptied(eng, counts, "T", i)
                if i == 0:
                    wait_alone(eng, parts_stored, b * (16 * PART_STORES) + BASE)
            value = b * 12 + (BASE + 3 * i + step)
            if eng == nc.scalar:
                eng.wait_ge(split_step, value)
            else:
                wait_alone(eng, split_step, value)
            if step == 0:
                ins = eng.tensor_tensor(rest[:], qkT[:, i, :], parts[:, i, 0, :], ALU.subtract)
            elif step == 2:
                ins = eng.tensor_tensor(parts[:, i, 2, :], rest[:], parts[:, i, 1, :], ALU.subtract)
            elif eng == nc.scalar:
                ins = eng.activation(parts[:, i, 1, :], rest[:], ACT.Copy)
            else:
                ins = eng.tensor_copy(parts[:, i, 1, :], rest[:])
            ins.then_inc(split_step, 1)

        block = ctx.enter_context(nc.Block())

        @block.sync
        def _(sp):
            for counter in (v_stored, qT_stored, parts_stored, st_stored, out_stored):
                sp.sem_inc(counter, BASE)
            sp.dma_start(w_in[:], ffn_w.rearrange("(k p) d -> p k d", p=P)).then_inc(w_loaded, 16)
            sp.dma_start(vr_in[:], ffn_v.rearrange("(k p) r -> p k r", p=P)).then_inc(w_loaded, 16)
            sp.dma_start(c_in[:], ffn_c.rearrange("(k p) r -> p k r", p=P)).then_inc(w_loaded, 16)
            sp.dma_start(w_qkv[:], w_attn.rearrange("(k p) n -> p k n", p=P)).then_inc(w_loaded, 16)
            sp.dma_start(w_out[:], w_proj.rearrange("(k p) n -> p k n", p=P)).then_inc(w_loaded, 16)
            sp.dma_start(bias_half[:], ffn_b.rearrange("(a n) -> a n", a=1).broadcast_to([P, DM])).then_inc(w_loaded, 16)
            sp.wait_ge(const_ready, 5)
            for b in range(BATCH):
                sp.dma_start(st_d[b, 0], st_new[:, 0, :]).then_inc(st_zero, 16)
            sp.wait_ge(st_zero, 16 * BATCH)
            sp.dma_start(x_sb[:], x_d[0:CH, :].rearrange("(i p) d -> p i d", p=P)).then_inc(x_loaded, 16)

            def load_kv(n, c, where=None):
                b, g = n // QUADS, n % QUADS
                a = b * CPB + c
                cols = slice(CH * c, CH * c + CH)
                where = kv_loaded[c] if where is None else where

                row = 0
                for q_part in range(SPLITS):
                    reps = sum(q == q_part for q, _ in PAIRS)
                    dst = slice(row, row + reps * HD)
                    src = part_d[bass.ds(a, 1), bass.ds((g % 2) * QH, QH), :, bass.ds(g // 2, 1)]
                    sp.dma_start(ks[dst, :, cols], src[:, :, 1, :, 0:reps].rearrange("o h g s d t -> (o g s d) h t")).then_inc(where, 16)
                    for r in range(reps):
                        sp.dma_start(qs[row + r * HD:row + r * HD + HD, :, cols],
                                     src[:, :, 0, :, q_part].rearrange("o h g d t -> (o g d) h t")).then_inc(where, 16)
                    row += reps * HD
                sp.dma_start(vt[:, NB * c:NB * c + NB, :],
                             v_d[bass.ds(a * CH, CH), bass.ds(g * QH * STRIP, QH * STRIP)]
                             .rearrange("(i p) n -> p i n", p=P)).then_inc(where, 16)
                sp.dma_start(qT[0:QH * HD, cols],
                             qT_d[bass.ds(a, 1), bass.ds(g * QH * HD, QH * HD), :]
                             .rearrange("o r t -> (o r) t")).then_inc(where, 16)
                sp.dma_start(st[:, NB * c:NB * c + NB, :],
                             st_d[bass.ds(b, 1), NB * c:NB * c + NB, :, bass.ds(g * QH * STRIP, QH * STRIP)]
                             .rearrange("o m r n -> (o r) m n")).then_inc(where, 16)

            def load_c(c, last, again=False):
                y_to, x1_to = c_bufs(c, last)[:2]
                token = (c - NCH) * CH if again else c * CH
                sp.dma_start(y_to[:], y_d[:, bass.ds(token, CH)].rearrange("(k p) t -> p k t", p=P)).then_inc(c_load(c, last)[0], 16)
                sp.dma_start(x1_to[:], x1_d[bass.ds(token, CH), :].rearrange("(i p) d -> p i d", p=P)).then_inc(c_load(c, last)[0], 16)

            def body(n, a, b, c, d, counts, prefetch=True, next_x=True, carry=True, again=False, last=False):
                a_store, v_store = (62, 26) if n is not None else (29, 37)
                for t in range(NHALF + 1):
                    if a is not None and next_x and t == a_store:
                        wait_emptied(sp, counts, "ffn", 1)
                        load_x(a + 1)
                    if c is not None and t == 8 and not last:
                        for i in range(2):
                            wait_alone(sp, y_stored[i], (c + BEHIND if n is not None else ITERS) * (16 * QH * CPB // 2))
                        load_c(c, last, again)
                    if last and c is not None and c + 1 < NCH and t == 8:
                        wait_alone(sp, emptied["dve"], counts.base("dve"))
                        load_c(c + 1, last)
                    if a is not None and t == a_store:
                        wait_emptied(sp, counts, "ffn", 1)
                        sp.dma_start(x1_d[bass.ds(a * CH, CH), :].rearrange("(i p) d -> p i d", p=P), x1[:]).then_inc(x1_stored, 16)
                    if b is not None and t == 20:
                        wait_alone(sp, st_stored, b * 16 + BASE)
                        sp.dma_start(st_new[:, 0, :], st_d[bass.ds(b // CPB, 1), bass.ds((b % CPB) * NB, 1), :, :]
                                     .rearrange("o m r n -> (o m r) n")).then_inc(st_loaded, 16)
                    if b is not None and t == v_store:
                        wait_emptied(sp, counts, "v", 1)
                        sp.dma_start(v_d[bass.ds(b * CH, CH), :].rearrange("(i p) n -> p i n", p=P),
                                     v_sb[:].rearrange("p i h s -> p i (h s)")).then_inc(v_stored, 16)
                    if b is not None and t == 43:
                        wait_emptied(sp, counts, "T", 1)
                        sp.dma_start(qT_d[bass.ds(b, 1), :, :].rearrange("o (g p) t -> (o p) g t", p=P),
                                     qkT[:, 0:2, :]).then_inc(qT_stored, 16)
                    if d is not None and t == 77:
                        wait_emptied(sp, counts, "out", 1)
                        token = (d - NCH) * CH if again else d * CH
                        sp.dma_start(out_d[bass.ds(token, CH), :].rearrange("(i p) d -> p i d", p=P), c_bufs(d, last)[2][:]).then_inc(out_stored, 16)
                    if b is not None and t == 58:
                        wait_alone(sp, split_step, b * 12 + (BASE + 12))
                        for h in range(P // HD):
                            sp.dma_start(part_d[bass.ds(b, 1), h].rearrange("o w g s d t -> (o d) (w g s) t"),
                                         parts[HD * h:HD * h + HD].rearrange("p g s t -> p (g s) t")).then_inc(parts_stored, 16)
                    if b is not None and t == 57:
                        wait_alone(sp, st_added, (b + 1) * NB)
                        sp.dma_start(st_d[bass.ds(b // CPB, 1), bass.ds((b % CPB) * NB + 1, NB), :, :]
                                     .rearrange("o m r n -> (o r) m n"), st_new[:, 1:NB + 1, :]).then_inc(st_stored, 16)
                    if n is not None:
                        for ci in range(CPB):
                            if t == COPY_AT[ci]:
                                store_y(n, ci)
                                if prefetch and ci > 0:
                                    load_kv(n + 1, CPB - 1 - ci)
                            if prefetch and t == 64 and ci == 0:
                                all_stored(b + 1 if b is not None else NCH)
                                load_kv(n + 1, CPB - 1)
                            if t == COPY_AT[ci] - NHALF and carry:
                                store_y(n - 1, ci)
                            if t == 9 and COPY_AT[ci] >= NHALF and carry:
                                load_kv(n, CPB - 1 - ci)

            def store_y(n, ci):
                wait_alone(sp, y_copied, n * CPB + (ci + 1))
                for h in range(QH):
                    sp.dma_start(y_d[bass.ds((n % QUADS) * QH * HD + h * HD, HD),
                                     bass.ds((n // QUADS) * SEQ + (CPB - 1 - ci) * CH, CH)],
                                 y_sb[ci % 2][STRIP * h:STRIP * h + HD, :]).then_inc(y_stored[ci % 2], 16)

            def all_stored(chunks):
                wait_alone(sp, v_stored, chunks * 16 + BASE)
                wait_alone(sp, qT_stored, chunks * 16 + BASE)
                wait_alone(sp, parts_stored, chunks * (16 * PART_STORES) + BASE)
                wait_alone(sp, st_stored, chunks * 16 + BASE)

            def early():
                all_stored(AHEAD - 1)
                load_kv(0, CPB - 2)

            def first():
                all_stored(AHEAD)
                for c in (CPB - 1, *range(CPB - 3, -1, -1)):
                    load_kv(0, c)

            def load_x(a):
                sp.dma_start(x_sb[:], x_d[bass.ds(a * CH, CH), :].rearrange("(i p) d -> p i d", p=P)).then_inc(x_loaded, 16)

            def drain():
                store_y(ITERS - 1, CPB - 1)
                for i in range(2):
                    sp.wait_ge(y_stored[i], ITERS * (16 * QH * CPB // 2))
                load_c(NCH - BEHIND, True)

            phases(sp, body, early, first, drain, prefetching=True)
            sp.wait_ge(out_stored, 16 * NCH + BASE)
            sp.wait_ge(x1_stored, 16 * NCH)
            for i in range(2):
                sp.wait_ge(y_stored[i], ITERS * (16 * QH * CPB // 2))

            def correct(n):
                for c in range(CPB):
                    load_kv(n, c, low_loaded)
                for ci in range(CPB):
                    strips = [(y_d[bass.ds((n % QUADS) * QH * HD + h * HD, HD), bass.ds((n // QUADS) * SEQ + (CPB - 1 - ci) * CH, CH)],
                               slice(STRIP * h, STRIP * h + HD)) for h in range(QH)]
                    for dram, rows in strips:
                        sp.dma_start(y_sb[0][rows, :], dram).then_inc(low_y_loaded, 16)
                    wait_alone(sp, low_added, n * CPB + (BASE + ci + 1))
                    for dram, rows in strips:
                        sp.dma_start(dram, y_sb[1][rows, :]).then_inc(low_stored, 16)
                    wait_alone(sp, low_stored, (n * CPB + (ci + 1)) * (16 * QH))

            lows(sp, correct, body)

        @block.gpsimd
        def _(pool):
            pool.memset(ident[:], 0.0).then_inc(const_ready, 1)
            pool.memset(smask[:], SLOPE * SCALE).then_inc(const_ready, 1)
            pool.memset(st_new[:], 0.0).then_inc(const_ready, 1)
            pool.memset(v_sb[:], 0.0).then_inc(const_ready, 1)
            pool.memset(ones[:], 1.0).then_inc(const_ready, 1)
            pool.memset(qT[:], 1.0).then_inc(const_ready, 1)
            pool.wait_ge(const_ready, 6)
            pool.affine_select(out=ident[:], in_=ident[:], compare_op=ALU.not_equal, fill=1.0, base=0,
                               pattern=[[-1, P]], channel_multiplier=1).then_inc(const_ready, 1)
            rows = smask[0:QH * HD, :]
            pool.affine_select(out=rows, in_=rows, compare_op=ALU.is_ge, fill=0.0, base=0,
                               pattern=[[0, QUADS], [-HD, QH], [0, HD]], channel_multiplier=1).then_inc(const_ready, 1)
            pool.wait_ge(const_ready, 8)
            pool.affine_select(out=rows, in_=rows, compare_op=ALU.is_ge, fill=0.0, base=HD - 1,
                               pattern=[[0, QUADS], [HD, QH], [0, HD]], channel_multiplier=-1).then_inc(const_ready, 1)
            pool.memset(smask[QH * HD:QH * HD + 1, :], 1.0).then_inc(const_ready, 1)
            pool.wait_ge(w_loaded, 16 * 6)
            pool.wait_ge(const_ready, 10)
            pool.tensor_scalar(bias_half[:], bias_half[:], 0.5, 0.0, ALU.mult, ALU.add).then_inc(const_ready, 1)
            pool.wait_ge(const_ready, CONSTS)

            def normalise(k, src, dst, value, i, own=None):
                own = own or k
                if i == 0:
                    wait_alone(pool, norm_ready[k], value)
                ins = pool.tensor_scalar(dst[:, i, :], src[:, i, :], rstd[own][:, i:i + 1], shift[own][:, i:i + 1],
                                         ALU.mult, ALU.add)
                if i == NB - 1:
                    ins.then_inc(z_ready[k], 1)

            def add_bias(k, x, ready, value, i):
                if i == 0:
                    wait_alone(pool, z_ready[k], value)
                ins = pool.tensor_tensor(x[:, i, :], x[:, i, :], bias_half[:], ALU.add)
                if i == NB - 1:
                    ins.then_inc(ready, 1)

            def body(n, a, b, c, d, counts, carry=True, again=False, last=False):
                ln_at = LN_EARLY if n is None else LN_AT
                for t in range(NHALF + 1):
                    if n is not None and t // 2 in DIAG:
                        m = DIAG.index(t // 2)
                        off = TILES[t // 2][3]
                        own_lin = lin[m % L_BUFS][:, 2 * (t % 2):2 * (t % 2) + 2, :]
                        own_poly = poly[2 * POLY_BUF[t // 2] + t % 2][:, :, off:off + P]
                        for buf, done, value in ((own_lin, lin_done, lin_made(n, t)),
                                                 (own_poly, poly_done, n * NHALF + (R_BUFS + t + 1))):
                            wait_alone(pool, done, value)
                            pool.affine_select(out=buf, in_=buf, compare_op=ALU.is_ge, fill=0.0, base=0,
                                               pattern=[[0, 2], [1, P]], channel_multiplier=-1).then_inc(masked, 1)
                    if a is not None:
                        if 0 <= t - ln_at["ln1"] - NORM < NB:
                            normalise("ln1", x_sb, z, a + 1, t - ln_at["ln1"] - NORM)
                        if 0 <= t - ln_at["ln1"] - BIAS < NB:
                            add_bias("ln1", x_sb, xb_ready, a + 1, t - ln_at["ln1"] - BIAS)
                        if t == ln_at["ln2"] + NORM:
                            wait_alone(pool, job_done, counts.made("z1T", 1))
                        if 0 <= t - ln_at["ln2"] - NORM < NB:
                            normalise("ln2", x1, z, a + 1, t - ln_at["ln2"] - NORM)
                    if c is not None:
                        x2_c, z3_c, _, own = c_bufs(c, last)[2:]
                        if 0 <= t - ln_at["ln3"] - NORM < NB:
                            normalise("ln3", x2_c, z3_c, c + 1, t - ln_at["ln3"] - NORM, own)
                        if 0 <= t - ln_at["ln3"] - BIAS < NB:
                            add_bias("ln3", x2_c, x2b_ready, c + 1, t - ln_at["ln3"] - BIAS)
                    for _, kind, i, start, who in counts.jobs:
                        if n is not None and kind == "T" and t - empty_at(kind, start, who) in SPLIT[::2]:
                            split(pool, b, counts, i, 0 if t == empty_at(kind, start, who) + SPLIT[0] else 2)
                        if kind == "state" and t == min(empty_at(kind, start, who) + 1, NHALF):
                            if i == 0:
                                wait_alone(pool, st_loaded, (b + 1) * 16)
                            else:
                                wait_alone(pool, st_added, b * NB + i)
                            wait_emptied(pool, counts, "state", i)
                            heads = st_new[:].rearrange("r m (h s) -> r m h s", h=HEADS)[:, :, :, 0:HD]
                            pool.tensor_tensor(heads[:, i + 1], heads[:, i], st_add[i % 2][:].rearrange("r (h d) -> r h d", h=HEADS), ALU.add).then_inc(st_added, 1)

            phases(pool, body)

            def correct(n):
                for m, t in enumerate(DIAG):
                    for half in range(2):
                        off = TILES[t][3]
                        wait_alone(pool, low_ready, n * NHALF + (2 * t + half + 1))
                        buf = poly[0][:, :, off:off + P]
                        pool.affine_select(out=buf, in_=buf, compare_op=ALU.is_ge, fill=0.0, base=0,
                                           pattern=[[0, 2], [1, P]], channel_multiplier=-1).then_inc(low_masked, 1)

            lows(pool, correct, body)

        @block.scalar
        def _(act):
            act.sem_inc(relu_done, S_BUFS)
            act.sem_inc(lin_done, S_BUFS)
            act.wait_ge(setup_pe, 1)
            nc.scalar.activation(vrT[:], score[0][0:32, 0, 0:DM], ACT.Copy).then_inc(setup_act, 1)
            nc.scalar.activation(cT[:], score[0][0:32, 0, DM:2 * DM], ACT.Copy).then_inc(setup_act, 1)
            for k in range(KC):
                act.wait_ge(setup_pe, 2 + k)
                nc.scalar.activation(w_ffn[:, k, :], y_ps[k][:, 0:DM], ACT.Copy, scale=0.5).then_inc(setup_act, 1)
            act.wait_ge(const_ready, CONSTS)

            def root(k, value, own=None):
                own = own or k
                act.wait_ge(var_done[k], value)
                nc.scalar.activation(sd[own][:], var[own][:], ACT.Sqrt).then_inc(sd_done[k], 1)

            def empty(b, d, kind, i, src, last):
                done = emptied["act"]
                if kind in ("z1T", "z2T", "z3T"):
                    dst = c_bufs(d, last)[4] if kind == "z3T" else {"z1T": zT, "z2T": z2T}[kind]
                    nc.scalar.activation(dst[:, i, :], src[:], ACT.Copy).then_inc(done, 1)
                if kind == "qk":
                    nc.scalar.activation(qk_sb[:, i, :], src[:], ACT.Copy).then_inc(done, 1)
                if kind == "v":
                    if i == 0:
                        act.wait_ge(v_stored, b * 16 + BASE)
                    nc.scalar.activation(v_sb[:, 2 * i:2 * i + 2, :, 0:HD], src[:].rearrange("p (b h d) -> p b h d", b=2, h=HEADS),
                                         ACT.Copy).then_inc(done, 1)
                if kind == "T":
                    if i == 0:
                        act.wait_ge(qT_stored, b * 16 + BASE)
                        act.wait_ge(parts_stored, b * (16 * PART_STORES) + BASE)
                        act.wait_ge(bounded, b * (2 * KC) + BASE)
                    nc.scalar.activation(qkT[:, i, :], src[:], ACT.Copy)
                    nc.scalar.activation(parts[:, i, 0, :], src[:], ACT.Copy).then_inc(done, 1)

            def body(n, a, b, c, d, counts, carry=True, again=False, last=False):
                ln_at = LN_EARLY if n is None else LN_AT
                for t in range(NHALF + 1):
                    for k, (_, kind, i, start, who) in enumerate(counts.jobs):
                        if who == "act" and t == empty_at(kind, start, who):
                            act.wait_ge(job_done, counts.made(kind, i))
                            empty(b, d, kind, i, bank[k % 2], last)
                    if n is not None and t < NHALF:
                        ci, _, j, off = TILES[t // 2]
                        act.wait_ge(qk_done, n * NHALF + t + 1)
                        act.wait_ge(poly_done, n * NHALF + t + 1)
                        nc.scalar.activation(relu[t % R_BUFS][:, :, off:CH], score[t % S_BUFS][:, :, off:CH], ACT.Relu,
                                             scale=SCALE).then_inc(relu_done, 1)
                        if t // 2 in DIAG:
                            act.wait_ge(pv_done, pv_used(n, same_lin(t // 2), t // 2))
                            nc.scalar.activation(lin[DIAG.index(t // 2) % L_BUFS][:, 2 * (t % 2):2 * (t % 2) + 2, :],
                                                 score[t % S_BUFS][:, :, off:off + P], ACT.Copy,
                                                 scale=SLOPE * SCALE, bias=1.0).then_inc(lin_done, 1)
                    for _, kind, i, start, who in counts.jobs:
                        if n is not None and kind == "T" and t == empty_at(kind, start, who) + SPLIT[1]:
                            split(act, b, counts, i, 1)
                    for ci in range(CPB):
                        if n is not None and t == COPY_AT[ci]:
                            copy_y(n, ci)
                        if n is not None and t == COPY_AT[ci] - NHALF and carry:
                            copy_y(n - 1, ci)
                    if a is not None and t == ln_at["ln1"] + ROOT:
                        root("ln1", a + 1)
                    if a is not None and t == ln_at["ln2"] + ROOT:
                        root("ln2", a + 1)
                    if c is not None and t == ln_at["ln3"] + ROOT:
                        root("ln3", c + 1, c_bufs(c, last)[5])

            def copy_y(n, ci):
                act.wait_ge(pv_done, n * NT + (PV_BASE + LAST[ci] + 1))
                act.wait_ge(y_stored[ci % 2], n * (16 * QH * CPB // 2) + (ci // 2) * 16 * QH)
                nc.scalar.activation(y_sb[ci % 2][:], y_ps[ci % 2][:], ACT.Copy).then_inc(y_copied, 1)

            phases(act, body, drain=lambda: copy_y(ITERS - 1, CPB - 1))
            lows(act, lambda n: None, body)

        @block.vector
        def _(dve):
            dve.sem_inc(poly_done, R_BUFS)
            for counter in (bounded, split_step, low_added):
                dve.sem_inc(counter, BASE)
            dve.wait_ge(const_ready, CONSTS)

            def stats(k, own, src, value, i):
                nc.vector.bn_stats(bnst[own][:, i, :], src[:, i, :]).then_inc(stats_done[k], 1)

            def aggregate(k, own, value):
                wait_alone(dve, stats_done[k], (value + 1) * NB)
                for i in range(NB):
                    nc.vector.bn_aggr(mv[own][:, i, :], bnst[own][:, i, :]).then_inc(aggr_done[k], 1)
                dve.wait_ge(aggr_done[k], (value + 1) * NB)
                nc.vector.tensor_scalar(var[own][:], mv[own][:, :, 1], EPS, None, ALU.add).then_inc(var_done[k], 1)

            def scales(k, own, value):
                dve.wait_ge(sd_done[k], value + 1)
                nc.vector.reciprocal(rstd[own][:], sd[own][:]).then_inc(rstd_done[k], 1)
                dve.wait_ge(rstd_done[k], value + 1)
                nc.vector.scalar_tensor_tensor(shift[own][:], mv[own][:, :, 0], -1.0, rstd[own][:], ALU.mult, ALU.mult).then_inc(norm_ready[k], 1)

            def empty(a, b, c, d, kind, i, src, last, again):
                done = emptied["dve"]
                two = src[:].rearrange("p (b d) -> p b d", b=2)
                if kind == "ffn":
                    if i == 0:
                        dve.wait_ge(xb_ready, a + 1)
                        dve.wait_ge(x1_stored, a * 16)
                    nc.vector.tensor_tensor(x1[:, 2 * i:2 * i + 2, :], two, x_sb[:, 2 * i:2 * i + 2, :], ALU.add).then_inc(done, 1)
                if kind == "proj":
                    _, x1_c, x2_c = c_bufs(c, last)[:3]
                    if i == 0:
                        dve.wait_ge(*c_load(c, last, again))
                        if last and c > NCH - BEHIND:
                            dve.wait_ge(out_stored, (c - 1) * 16 + BASE)
                            dve.wait_ge(x1_stored, NCH * 16)
                        else:
                            dve.wait_ge(out_stored, c * 16 + BASE)
                    nc.vector.scalar_tensor_tensor(x2_c[:, 2 * i:2 * i + 2, :], two, 1.0 / DIVISOR, x1_c[:, 2 * i:2 * i + 2, :],
                                                   ALU.mult, ALU.add).then_inc(done, 1)
                if kind == "out":
                    x2_d = c_bufs(d, last)[2]
                    if i == 0:
                        dve.wait_ge(x2b_ready, d + 1)
                    nc.vector.tensor_tensor(x2_d[:, 2 * i:2 * i + 2, :], two, x2_d[:, 2 * i:2 * i + 2, :], ALU.add).then_inc(done, 1)
                if kind == "state":
                    if i >= 2:
                        dve.wait_ge(st_added, b * NB + i - 1)
                    nc.vector.tensor_tensor(st_add[i % 2][:], src[0:QH * HD + 1, 0:DM], smask[:], ALU.mult).then_inc(done, 1)

            def body(n, a, b, c, d, counts, carry=True, again=False, last=False):
                ln_at = LN_EARLY if n is None else LN_AT
                for t in range(NHALF + 1):
                    for k, (_, kind, i, start, who) in enumerate(counts.jobs):
                        if who == "dve" and t == empty_at(kind, start, who):
                            dve.wait_ge(job_done, counts.made(kind, i))
                            empty(a, b, c, d, kind, i, bank[k % 2], last, again)
                    if n is not None and t < NHALF:
                        ci, _, j, off = TILES[t // 2]
                        dve.wait_ge(relu_done, n * NHALF + (S_BUFS + t + 1))
                        if t % 2 == 0:
                            dve.wait_ge(pv_done, pv_used(n, same_poly(t // 2), t // 2))
                        r = relu[t % R_BUFS][:, :, off:CH]
                        nc.vector.scalar_tensor_tensor(poly[2 * POLY_BUF[t // 2] + t % 2][:, :, off:CH], r, -SLOPE, r,
                                                       ALU.add, ALU.mult).then_inc(poly_done, 1)
                    for _, kind, i, start, who in counts.jobs:
                        if kind == "T" and t == empty_at(kind, start, who) + 1:
                            wait_emptied(dve, counts, "T", i)
                            nc.vector.tensor_reduce(qk_max[:, bass.ds(b, 1), i:i + 1].rearrange("p c g -> p (c g)"), qkT[:, i, :],
                                                    AX.X, ALU.max, apply_absolute_value=True).then_inc(bounded, 1)
                            if n is None:
                                for step in range(3):
                                    split(dve, b, counts, i, step)
                    x2_c, _, _, own_c = c_bufs(c, last)[2:] if c is not None else [None] * 4
                    for k, chunk, x, own in (("ln1", a, x_sb, "ln1"), ("ln2", a, x1, "ln2"), ("ln3", c, x2_c, own_c)):
                        if chunk is None:
                            continue
                        step = t - ln_at[k]
                        if step == 0:
                            if k == "ln1":
                                dve.wait_ge(x_loaded, (a + 1) * 16)
                            else:
                                wait_emptied(dve, counts, "ffn" if k == "ln2" else "proj", 1)
                        if 0 <= step < NB:
                            stats(k, own, x, chunk, step)
                        if step == AGGR:
                            aggregate(k, own, chunk)
                        if step == SCALES:
                            scales(k, own, chunk)

            phases(dve, body)

            dve.wait_ge(bounded, NCH * 2 * KC + BASE)
            nc.vector.tensor_reduce(qk_top[:], qk_max[:].rearrange("p c g -> p g c"), AX.X, ALU.max).then_inc(bound_ready, 1)
            dve.wait_ge(bound_ready, 1)
            nc.vector.tensor_tensor(qk_prod[:], qk_top[:, 0:KC], qk_top[:, KC:2 * KC], ALU.mult).then_inc(bound_step, 1)
            dve.wait_ge(bound_transposed, 1)
            nc.vector.tensor_reduce(head_bound[:], bank[0][0:1, 0:DM].rearrange("p (h d) -> p h d", h=HEADS), AX.X, ALU.add).then_inc(bound_ready, 1)
            dve.wait_ge(bound_ready, 2)
            nc.vector.tensor_reduce(bound[:], head_bound[:], AX.X, ALU.max).then_inc(bound_ready, 1)
            dve.wait_ge(bound_ready, 3)
            nc.vector.tensor_scalar(no_low[:], bound[:], BOUND, None, ALU.is_lt).then_inc(bound_ready, 1)

            def correct(n):
                for h in range(NHALF):
                    ci, c, j, off = TILES[h // 2]
                    s = score[0][:, :, off:CH]
                    dve.wait_ge(low_scored, n * NHALF + (h + 1))
                    nc.vector.tensor_scalar(relu[0][:, :, off:CH], s, -SLOPE * SCALE, -1.0, ALU.mult, ALU.add).then_inc(low_line, 1)
                    dve.wait_ge(low_line, n * NHALF + (h + 1))
                    nc.vector.scalar_tensor_tensor(poly[0][:, :, off:CH], s, X_INT / SCALE, relu[0][:, :, off:CH],
                                                   ALU.is_lt, ALU.mult).then_inc(low_ready, 1)
                    if h == 2 * LAST[ci] + 1:
                        dve.wait_ge(low_summed, n * CPB + (ci + 1))
                        dve.wait_ge(low_y_loaded, (n * CPB + (ci + 1)) * (16 * QH))
                        nc.vector.tensor_tensor(y_sb[1][:], y_ps[0][:], y_sb[0][:], ALU.add).then_inc(low_added, 1)

            lows(dve, correct, body)

        @block.tensor
        def _(pe):
            def mm(*args, start=True, stop=True):
                return nc.tensor.matmul(*args, start=start, stop=stop, skip_group_check=True)

            pe.sem_inc(pv_done, PV_BASE)
            pe.wait_ge(const_ready, CONSTS)
            pe.wait_ge(w_loaded, 16 * 6)
            for k in range(KC):
                nc.tensor.transpose(score[0][0:32, 0, P * k:P * k + P], vr_in[:, k, :], ident[:])
                ins = nc.tensor.transpose(score[0][0:32, 0, DM + P * k:DM + P * k + P], c_in[:, k, :], ident[:])
            ins.then_inc(setup_pe, 1)
            pe.wait_ge(setup_act, 2)
            for k in range(KC):
                for o in range(KC):
                    dst = y_ps[k][:, P * o:P * o + P]
                    mm(dst, w_in[:, o, P * k:P * k + P], ident[:], start=True, stop=False)
                    ins = mm(dst, vrT[:, P * k:P * k + P], cT[:, P * o:P * o + P], start=False, stop=True)
                ins.then_inc(setup_pe, 1)
            pe.wait_ge(setup_act, 4)

            def transposes(dst, src, i):
                for blk in range(NB):
                    ins = nc.tensor.transpose(dst[:, P * blk:P * blk + P], src[:, blk, P * i:P * i + P], ident[:])
                return ins

            def job(a, b, c, d, counts, k, kind, i, piece, last, again):
                dst = bank[k % 2]
                if piece == 0:
                    if k < 2:
                        for who in ("act", "dve"):
                            pe.wait_ge(emptied[who], counts.base(who))
                    else:
                        wait_emptied(pe, counts, counts.jobs[k - 2][1], counts.jobs[k - 2][2])
                first = piece == 0 and i == 0
                half = dst[:, DM * (piece // 2):DM * (piece // 2) + DM]
                kc = piece % 2
                if kind in ("z1T", "z2T", "z3T"):
                    name = {"z1T": "ln1", "z2T": "ln2", "z3T": "ln3"}[kind]
                    if first:
                        pe.wait_ge(z_ready[name], (d if kind == "z3T" else a) + 1)
                    ins = transposes(dst, c_bufs(d, last)[3] if kind == "z3T" else z, i)
                if kind in ("ffn", "out", "proj", "v"):
                    if first and kind == "proj":
                        pe.wait_ge(*c_load(c, last, again))
                    if first and kind in ("ffn", "out"):
                        wait_emptied(pe, counts, {"ffn": "z1T", "out": "z3T"}[kind], 1)
                    w = {"ffn": w_ffn, "out": w_ffn, "proj": w_out, "v": w_qkv[:, :, 2 * DM:]}[kind]
                    src = {"ffn": lambda: zT, "out": lambda: c_bufs(d, last)[4], "proj": lambda: c_bufs(c, last)[0],
                           "v": lambda: z2T}[kind]()
                    blk = 2 * i + piece // 2
                    ins = mm(half, src[:, kc, P * blk:P * blk + P], w[:, kc, :], start=kc == 0, stop=kc == KC - 1)
                if kind == "qk":
                    if first:
                        pe.wait_ge(emptied["act"], counts.base("act"))
                    cols = slice(DM * (piece // 2), DM * (piece // 2) + DM)
                    ins = mm(half, z2T[:, kc, P * i:P * i + P], w_qkv[:, kc, cols], start=kc == 0, stop=kc == KC - 1)
                if kind == "T":
                    if first:
                        wait_emptied(pe, counts, "qk", 3)
                    ins = transposes(dst, qk_sb, i)
                if kind == "state":
                    if first:
                        wait_emptied(pe, counts, "v", 1)
                    if piece == 0:
                        for g in range(QUADS):
                            k_cols = qk_sb[:, i, DM + QH * HD * g:DM + QH * HD * (g + 1)]
                            ins = mm(dst[0:QH * HD, QH * HD * g:QH * HD * (g + 1)], k_cols, v_sb[:, i, QH * g:QH * g + QH, 0:HD])
                    else:
                        ins = mm(dst[QH * HD:QH * HD + 1, 0:DM], ones[:], v_sb[:, i, :, 0:HD])
                if piece == PIECES[kind] - 1:
                    ins.then_inc(job_done, 1)

            def score_half(n, h):
                ci, c, j, off = TILES[h // 2]
                if h % 2 == 0 and j // NB not in [x[2] // NB for x in TILES[:h // 2]]:
                    pe.wait_ge(kv_loaded[j // NB], (n + 1) * (16 * KV_LOADS))
                pe.wait_ge(relu_done, n * NHALF + h + 1)
                if h < S_BUFS:
                    pe.wait_ge(lin_done, n * 2 * len(DIAG) + h + 1)
                elif (h - S_BUFS) // 2 in DIAG:
                    pe.wait_ge(lin_done, lin_made(n, h - S_BUFS))
                for u in range(2):
                    head = 2 * (h % 2) + u
                    ins = mm(score[h % S_BUFS][:, u, off:CH], ks[:, head, P * j:P * j + P],
                             qs[:, head, CH * c + off:CH * c + CH])
                ins.then_inc(qk_done, 1)

            def values(n, t):
                ci, c, j, off = TILES[t]
                y = y_ps[ci % 2]
                if t == FIRST[ci]:
                    if ci >= 2 or not (isinstance(n, int) and n == 0):
                        pe.wait_ge(y_copied, n * CPB + (ci - 1))
                    for m in range(NB):
                        mm(y[:, P * m:P * m + P], st[:, NB * c + m, :], qT[:, CH * c + P * m:CH * c + P * m + P],
                           start=m == 0, stop=False)
                if t in DIAG:
                    pe.wait_ge(masked, n * 4 * len(DIAG) + (4 * DIAG.index(t) + 4))
                else:
                    pe.wait_ge(poly_done, n * NHALF + (R_BUFS + 2 * t + 2))
                last = t == LAST[ci]
                for head in range(QH):
                    ins = mm(y[STRIP * head:STRIP * head + HD, off:CH], vt[:, j, STRIP * head:STRIP * head + HD],
                             poly[2 * POLY_BUF[t] + head // 2][:, head % 2, off:CH], start=False, stop=last)
                if t in DIAG:
                    for head in range(QH):
                        ins = mm(y[STRIP * head:STRIP * head + HD, off:off + P], vt[:, j, STRIP * head:STRIP * head + HD],
                                 lin[DIAG.index(t) % L_BUFS][:, head, :], start=False, stop=False)
                ins.then_inc(pv_done, 1)

            def body(n, a, b, c, d, counts, carry=True, again=False, last=False):
                ln_at = LN_EARLY if n is None else LN_AT
                for t in range(NHALF):
                    if n is not None:
                        score_half(n, t)
                        if t % 2 == 0 and t // 2 >= LAG:
                            values(n, t // 2 - LAG)
                        elif t % 2 == 0 and carry:
                            values(n - 1, t // 2 - LAG + NT)
                    for k, (_, kind, i, start, _) in enumerate(counts.jobs):
                        if 0 <= t - start < PIECES[kind]:
                            job(a, b, c, d, counts, k, kind, i, t - start, last, again)

            def drain():
                for t in range(NT - LAG, NT):
                    values(ITERS - 1, t)

            phases(pe, body, drain=drain)

            pe.wait_ge(bound_step, 1)
            for who, jobs in (("act", sum(x[4] == "act" for x in JOBS)), ("dve", sum(x[4] == "dve" for x in JOBS))):
                pe.wait_ge(emptied[who], NCH * jobs)
            for g in range(KC):
                ins = nc.tensor.transpose(bank[0][0:1, P * g:P * g + P], qk_prod[:, g:g + 1], ident[:])
            ins.then_inc(bound_transposed, 1)

            def correct(n):
                pe.wait_ge(low_loaded, (n + 1) * (16 * KV_LOADS * CPB))
                for h in range(NHALF):
                    ci, c, j, off = TILES[h // 2]
                    y = y_ps[0]
                    if h == 2 * FIRST[ci]:
                        pe.wait_ge(low_added, n * CPB + (BASE + ci))
                        mm(y[:], st[:, 0, :], qT[:, 0:CH], start=True, stop=False)
                    for u in range(2):
                        head = 2 * (h % 2) + u
                        ins = mm(score[0][:, u, off:CH], ks[:, head, P * j:P * j + P], qs[:, head, CH * c + off:CH * c + CH])
                    ins.then_inc(low_scored, 1)
                    pe.wait_ge(low_ready, n * NHALF + (h + 1))
                    if h // 2 in DIAG:
                        pe.wait_ge(low_masked, n * (2 * len(DIAG)) + (2 * DIAG.index(h // 2) + h % 2 + 1))
                    for u in range(2):
                        head = 2 * (h % 2) + u
                        ins = mm(y[STRIP * head:STRIP * head + HD, off:CH], vt[:, j, STRIP * head:STRIP * head + HD],
                                 poly[0][:, u, off:CH], start=False, stop=h == 2 * LAST[ci] + 1)
                    if h == 2 * LAST[ci] + 1:
                        ins.then_inc(low_summed, 1)

            lows(pe, correct, body)


_INS = ['L0_attn_x', 'L0_attn_W_attn', 'L0_attn_W_proj', 'L0_ffn_W', 'L0_ffn_b', 'L0_ffn_V_r', 'L0_ffn_C']
_OUTS = [((BATCH, SEQ, DM), 'float32')]


def kernel(**inputs):
    import numpy as _np
    import concourse.bacc as _bacc
    from concourse import mybir as _mybir
    from concourse.bass_utils import run_bass_kernel_spmd as _run

    nc = _bacc.Bacc("TRN2", target_bir_lowering=False, num_devices=1)
    arrays, args = {}, []
    for name in _INS:
        a = _np.ascontiguousarray(inputs[name])
        arrays[f"in_{name}_dram"] = a
        args.append(nc.dram_tensor(f"in_{name}_dram", a.shape, _mybir.dt.from_np(a.dtype), kind="ExternalInput").ap())
    for i, (shape, dtype) in enumerate(_OUTS):
        dt = _mybir.dt.from_np(_np.dtype(dtype))
        args.append(nc.dram_tensor(f"out_{i}_dram", shape, dt, kind="ExternalOutput").ap())
    build(nc, *args)
    r = _run(nc, [arrays], core_ids=[0])
    return r.results[0]["out_0_dram"]
```
